# Optimizing a Trainium2 kernel written in Bass

```python
import numpy as np
import jax
import jax.numpy as jnp

def _softmax(x, axis=-1):
    return jax.nn.softmax(x, axis=axis)

def _gelu(x):
    return jax.nn.gelu(x, approximate=True)

def _silu(x):
    return jax.nn.silu(x)

def _sigmoid(x):
    return jax.nn.sigmoid(x)

def _layernorm(x, axis=-1, eps=1e-05):
    m = jnp.mean(x, axis=axis, keepdims=True)
    v = jnp.var(x, axis=axis, keepdims=True)
    return (x - m) / jnp.sqrt(v + eps)

def _scatter_add(tgt, idx, src, axis=0):
    return tgt.at[idx].add(src)

def _segment_sum(src, seg, n):
    return jax.ops.segment_sum(src, seg, n)
kernel_name = 'mk_rec_standalone_d1_rec_r8_527e33'

def setup_inputs(seed: int=0):
    np.random.seed(seed)
    _w = jnp.asarray

    def _rec_inputs():
        import jax
        import jax.numpy as jnp
        _rk = jax.random.key(seed)
        r_uid = jax.random.randint(jax.random.fold_in(_rk, 1), (512,), 72, 99964, jnp.int32)
        r_mid = jax.random.randint(jax.random.fold_in(_rk, 2), (512,), 297, 998633, jnp.int32)
        r_cat = jax.random.randint(jax.random.fold_in(_rk, 3), (512,), 0, 998, jnp.int32)
        r_historical_mid = jnp.stack([jax.random.randint(jax.random.fold_in(jax.random.fold_in(_rk, 4), 0), (512,), 419, 999446, jnp.int32), jax.random.randint(jax.random.fold_in(jax.random.fold_in(_rk, 4), 1), (512,), 38, 999969, jnp.int32), jax.random.randint(jax.random.fold_in(jax.random.fold_in(_rk, 4), 2), (512,), 1969, 124761, jnp.int32), jax.random.randint(jax.random.fold_in(jax.random.fold_in(_rk, 4), 3), (512,), 487, 999797, jnp.int32), jax.random.randint(jax.random.fold_in(jax.random.fold_in(_rk, 4), 4), (512,), 1312, 124924, jnp.int32), jax.random.randint(jax.random.fold_in(jax.random.fold_in(_rk, 4), 5), (512,), 982, 999172, jnp.int32), jax.random.randint(jax.random.fold_in(jax.random.fold_in(_rk, 4), 6), (512,), 636, 999989, jnp.int32), jax.random.randint(jax.random.fold_in(jax.random.fold_in(_rk, 4), 7), (512,), 1174, 998009, jnp.int32), jax.random.randint(jax.random.fold_in(jax.random.fold_in(_rk, 4), 8), (512,), 1830, 997796, jnp.int32), jax.random.randint(jax.random.fold_in(jax.random.fold_in(_rk, 4), 9), (512,), 1364, 999005, jnp.int32), jax.random.randint(jax.random.fold_in(jax.random.fold_in(_rk, 4), 10), (512,), 385, 999921, jnp.int32), jax.random.randint(jax.random.fold_in(jax.random.fold_in(_rk, 4), 11), (512,), 1861, 999457, jnp.int32), jax.random.randint(jax.random.fold_in(jax.random.fold_in(_rk, 4), 12), (512,), 312, 999813, jnp.int32), jax.random.randint(jax.random.fold_in(jax.random.fold_in(_rk, 4), 13), (512,), 1292, 998622, jnp.int32), jax.random.randint(jax.random.fold_in(jax.random.fold_in(_rk, 4), 14), (512,), 227, 999366, jnp.int32), jax.random.randint(jax.random.fold_in(jax.random.fold_in(_rk, 4), 15), (512,), 6, 124978, jnp.int32), jax.random.randint(jax.random.fold_in(jax.random.fold_in(_rk, 4), 16), (512,), 66, 999799, jnp.int32), jax.random.randint(jax.random.fold_in(jax.random.fold_in(_rk, 4), 17), (512,), 135, 999630, jnp.int32), jax.random.randint(jax.random.fold_in(jax.random.fold_in(_rk, 4), 18), (512,), 790, 124973, jnp.int32), jax.random.randint(jax.random.fold_in(jax.random.fold_in(_rk, 4), 19), (512,), 1951, 999667, jnp.int32), jax.random.randint(jax.random.fold_in(jax.random.fold_in(_rk, 4), 20), (512,), 200, 999413, jnp.int32), jax.random.randint(jax.random.fold_in(jax.random.fold_in(_rk, 4), 21), (512,), 527, 999105, jnp.int32), jax.random.randint(jax.random.fold_in(jax.random.fold_in(_rk, 4), 22), (512,), 3171, 999978, jnp.int32), jax.random.randint(jax.random.fold_in(jax.random.fold_in(_rk, 4), 23), (512,), 2377, 998385, jnp.int32), jax.random.randint(jax.random.fold_in(jax.random.fold_in(_rk, 4), 24), (512,), 355, 999314, jnp.int32), jax.random.randint(jax.random.fold_in(jax.random.fold_in(_rk, 4), 25), (512,), 53, 999910, jnp.int32), jax.random.randint(jax.random.fold_in(jax.random.fold_in(_rk, 4), 26), (512,), 2179, 124828, jnp.int32), jax.random.randint(jax.random.fold_in(jax.random.fold_in(_rk, 4), 27), (512,), 204, 999372, jnp.int32), jax.random.randint(jax.random.fold_in(jax.random.fold_in(_rk, 4), 28), (512,), 568, 997425, jnp.int32), jax.random.randint(jax.random.fold_in(jax.random.fold_in(_rk, 4), 29), (512,), 541, 998315, jnp.int32), jax.random.randint(jax.random.fold_in(jax.random.fold_in(_rk, 4), 30), (512,), 959, 999892, jnp.int32), jax.random.randint(jax.random.fold_in(jax.random.fold_in(_rk, 4), 31), (512,), 26, 999709, jnp.int32), jax.random.randint(jax.random.fold_in(jax.random.fold_in(_rk, 4), 32), (512,), 74, 999511, jnp.int32), jax.random.randint(jax.random.fold_in(jax.random.fold_in(_rk, 4), 33), (512,), 1313, 997180, jnp.int32), jax.random.randint(jax.random.fold_in(jax.random.fold_in(_rk, 4), 34), (512,), 369, 999836, jnp.int32), jax.random.randint(jax.random.fold_in(jax.random.fold_in(_rk, 4), 35), (512,), 150, 999746, jnp.int32), jax.random.randint(jax.random.fold_in(jax.random.fold_in(_rk, 4), 36), (512,), 1877, 124981, jnp.int32), jax.random.randint(jax.random.fold_in(jax.random.fold_in(_rk, 4), 37), (512,), 2362, 999959, jnp.int32), jax.random.randint(jax.random.fold_in(jax.random.fold_in(_rk, 4), 38), (512,), 447, 999958, jnp.int32), jax.random.randint(jax.random.fold_in(jax.random.fold_in(_rk, 4), 39), (512,), 89, 999884, jnp.int32), jax.random.randint(jax.random.fold_in(jax.random.fold_in(_rk, 4), 40), (512,), 557, 999483, jnp.int32), jax.random.randint(jax.random.fold_in(jax.random.fold_in(_rk, 4), 41), (512,), 640, 999902, jnp.int32), jax.random.randint(jax.random.fold_in(jax.random.fold_in(_rk, 4), 42), (512,), 288, 999401, jnp.int32), jax.random.randint(jax.random.fold_in(jax.random.fold_in(_rk, 4), 43), (512,), 376, 999986, jnp.int32), jax.random.randint(jax.random.fold_in(jax.random.fold_in(_rk, 4), 44), (512,), 412, 999406, jnp.int32), jax.random.randint(jax.random.fold_in(jax.random.fold_in(_rk, 4), 45), (512,), 36, 999732, jnp.int32), jax.random.randint(jax.random.fold_in(jax.random.fold_in(_rk, 4), 46), (512,), 654, 997679, jnp.int32), jax.random.randint(jax.random.fold_in(jax.random.fold_in(_rk, 4), 47), (512,), 2931, 998678, jnp.int32), jax.random.randint(jax.random.fold_in(jax.random.fold_in(_rk, 4), 48), (512,), 768, 999593, jnp.int32), jax.random.randint(jax.random.fold_in(jax.random.fold_in(_rk, 4), 49), (512,), 4103, 999845, jnp.int32), jax.random.randint(jax.random.fold_in(jax.random.fold_in(_rk, 4), 50), (512,), 732, 998190, jnp.int32), jax.random.randint(jax.random.fold_in(jax.random.fold_in(_rk, 4), 51), (512,), 66, 999794, jnp.int32), jax.random.randint(jax.random.fold_in(jax.random.fold_in(_rk, 4), 52), (512,), 399, 999829, jnp.int32), jax.random.randint(jax.random.fold_in(jax.random.fold_in(_rk, 4), 53), (512,), 51, 999223, jnp.int32), jax.random.randint(jax.random.fold_in(jax.random.fold_in(_rk, 4), 54), (512,), 55, 999765, jnp.int32), jax.random.randint(jax.random.fold_in(jax.random.fold_in(_rk, 4), 55), (512,), 789, 124954, jnp.int32), jax.random.randint(jax.random.fold_in(jax.random.fold_in(_rk, 4), 56), (512,), 2791, 997377, jnp.int32), jax.random.randint(jax.random.fold_in(jax.random.fold_in(_rk, 4), 57), (512,), 550, 124601, jnp.int32), jax.random.randint(jax.random.fold_in(jax.random.fold_in(_rk, 4), 58), (512,), 1954, 999180, jnp.int32), jax.random.randint(jax.random.fold_in(jax.random.fold_in(_rk, 4), 59), (512,), 2591, 999854, jnp.int32), jax.random.randint(jax.random.fold_in(jax.random.fold_in(_rk, 4), 60), (512,), 428, 999327, jnp.int32), jax.random.randint(jax.random.fold_in(jax.random.fold_in(_rk, 4), 61), (512,), 1228, 997009, jnp.int32), jax.random.randint(jax.random.fold_in(jax.random.fold_in(_rk, 4), 62), (512,), 466, 998562, jnp.int32), jax.random.randint(jax.random.fold_in(jax.random.fold_in(_rk, 4), 63), (512,), 532, 998538, jnp.int32), jax.random.randint(jax.random.fold_in(jax.random.fold_in(_rk, 4), 64), (512,), 174, 998862, jnp.int32), jax.random.randint(jax.random.fold_in(jax.random.fold_in(_rk, 4), 65), (512,), 951, 996205, jnp.int32), jax.random.randint(jax.random.fold_in(jax.random.fold_in(_rk, 4), 66), (512,), 409, 999531, jnp.int32), jax.random.randint(jax.random.fold_in(jax.random.fold_in(_rk, 4), 67), (512,), 449, 999793, jnp.int32), jax.random.randint(jax.random.fold_in(jax.random.fold_in(_rk, 4), 68), (512,), 807, 999481, jnp.int32), jax.random.randint(jax.random.fold_in(jax.random.fold_in(_rk, 4), 69), (512,), 518, 997969, jnp.int32), jax.random.randint(jax.random.fold_in(jax.random.fold_in(_rk, 4), 70), (512,), 337, 999753, jnp.int32), jax.random.randint(jax.random.fold_in(jax.random.fold_in(_rk, 4), 71), (512,), 258, 997575, jnp.int32), jax.random.randint(jax.random.fold_in(jax.random.fold_in(_rk, 4), 72), (512,), 1306, 124981, jnp.int32), jax.random.randint(jax.random.fold_in(jax.random.fold_in(_rk, 4), 73), (512,), 448, 999934, jnp.int32), jax.random.randint(jax.random.fold_in(jax.random.fold_in(_rk, 4), 74), (512,), 223, 124979, jnp.int32), jax.random.randint(jax.random.fold_in(jax.random.fold_in(_rk, 4), 75), (512,), 12, 999587, jnp.int32), jax.random.randint(jax.random.fold_in(jax.random.fold_in(_rk, 4), 76), (512,), 220, 999806, jnp.int32), jax.random.randint(jax.random.fold_in(jax.random.fold_in(_rk, 4), 77), (512,), 70, 999929, jnp.int32), jax.random.randint(jax.random.fold_in(jax.random.fold_in(_rk, 4), 78), (512,), 343, 999507, jnp.int32), jax.random.randint(jax.random.fold_in(jax.random.fold_in(_rk, 4), 79), (512,), 1031, 998900, jnp.int32), jax.random.randint(jax.random.fold_in(jax.random.fold_in(_rk, 4), 80), (512,), 896, 999764, jnp.int32), jax.random.randint(jax.random.fold_in(jax.random.fold_in(_rk, 4), 81), (512,), 48, 998947, jnp.int32), jax.random.randint(jax.random.fold_in(jax.random.fold_in(_rk, 4), 82), (512,), 1279, 999460, jnp.int32), jax.random.randint(jax.random.fold_in(jax.random.fold_in(_rk, 4), 83), (512,), 461, 999357, jnp.int32), jax.random.randint(jax.random.fold_in(jax.random.fold_in(_rk, 4), 84), (512,), 974, 999355, jnp.int32), jax.random.randint(jax.random.fold_in(jax.random.fold_in(_rk, 4), 85), (512,), 158, 998890, jnp.int32), jax.random.randint(jax.random.fold_in(jax.random.fold_in(_rk, 4), 86), (512,), 246, 998002, jnp.int32), jax.random.randint(jax.random.fold_in(jax.random.fold_in(_rk, 4), 87), (512,), 371, 124858, jnp.int32), jax.random.randint(jax.random.fold_in(jax.random.fold_in(_rk, 4), 88), (512,), 1310, 999753, jnp.int32), jax.random.randint(jax.random.fold_in(jax.random.fold_in(_rk, 4), 89), (512,), 119, 999502, jnp.int32), jax.random.randint(jax.random.fold_in(jax.random.fold_in(_rk, 4), 90), (512,), 231, 996419, jnp.int32), jax.random.randint(jax.random.fold_in(jax.random.fold_in(_rk, 4), 91), (512,), 1868, 999626, jnp.int32), jax.random.randint(jax.random.fold_in(jax.random.fold_in(_rk, 4), 92), (512,), 236, 124751, jnp.int32), jax.random.randint(jax.random.fold_in(jax.random.fold_in(_rk, 4), 93), (512,), 139, 999055, jnp.int32), jax.random.randint(jax.random.fold_in(jax.random.fold_in(_rk, 4), 94), (512,), 331, 999951, jnp.int32), jax.random.randint(jax.random.fold_in(jax.random.fold_in(_rk, 4), 95), (512,), 296, 124960, jnp.int32), jax.random.randint(jax.random.fold_in(jax.random.fold_in(_rk, 4), 96), (512,), 1790, 999823, jnp.int32), jax.random.randint(jax.random.fold_in(jax.random.fold_in(_rk, 4), 97), (512,), 1649, 124949, jnp.int32), jax.random.randint(jax.random.fold_in(jax.random.fold_in(_rk, 4), 98), (512,), 377, 999502, jnp.int32), jax.random.randint(jax.random.fold_in(jax.random.fold_in(_rk, 4), 99), (512,), 1870, 999985, jnp.int32), jax.random.randint(jax.random.fold_in(jax.random.fold_in(_rk, 4), 100), (512,), 226, 997941, jnp.int32), jax.random.randint(jax.random.fold_in(jax.random.fold_in(_rk, 4), 101), (512,), 388, 998897, jnp.int32), jax.random.randint(jax.random.fold_in(jax.random.fold_in(_rk, 4), 102), (512,), 1600, 999911, jnp.int32), jax.random.randint(jax.random.fold_in(jax.random.fold_in(_rk, 4), 103), (512,), 1094, 999692, jnp.int32), jax.random.randint(jax.random.fold_in(jax.random.fold_in(_rk, 4), 104), (512,), 503, 999219, jnp.int32), jax.random.randint(jax.random.fold_in(jax.random.fold_in(_rk, 4), 105), (512,), 547, 999423, jnp.int32), jax.random.randint(jax.random.fold_in(jax.random.fold_in(_rk, 4), 106), (512,), 983, 995561, jnp.int32), jax.random.randint(jax.random.fold_in(jax.random.fold_in(_rk, 4), 107), (512,), 1293, 999581, jnp.int32), jax.random.randint(jax.random.fold_in(jax.random.fold_in(_rk, 4), 108), (512,), 999, 999887, jnp.int32), jax.random.randint(jax.random.fold_in(jax.random.fold_in(_rk, 4), 109), (512,), 264, 999676, jnp.int32), jax.random.randint(jax.random.fold_in(jax.random.fold_in(_rk, 4), 110), (512,), 521, 999341, jnp.int32), jax.random.randint(jax.random.fold_in(jax.random.fold_in(_rk, 4), 111), (512,), 82, 999001, jnp.int32), jax.random.randint(jax.random.fold_in(jax.random.fold_in(_rk, 4), 112), (512,), 3521, 999481, jnp.int32), jax.random.randint(jax.random.fold_in(jax.random.fold_in(_rk, 4), 113), (512,), 127, 999182, jnp.int32), jax.random.randint(jax.random.fold_in(jax.random.fold_in(_rk, 4), 114), (512,), 428, 999363, jnp.int32), jax.random.randint(jax.random.fold_in(jax.random.fold_in(_rk, 4), 115), (512,), 131, 998428, jnp.int32), jax.random.randint(jax.random.fold_in(jax.random.fold_in(_rk, 4), 116), (512,), 871, 999428, jnp.int32), jax.random.randint(jax.random.fold_in(jax.random.fold_in(_rk, 4), 117), (512,), 731, 999756, jnp.int32), jax.random.randint(jax.random.fold_in(jax.random.fold_in(_rk, 4), 118), (512,), 154, 999183, jnp.int32), jax.random.randint(jax.random.fold_in(jax.random.fold_in(_rk, 4), 119), (512,), 1040, 999399, jnp.int32), jax.random.randint(jax.random.fold_in(jax.random.fold_in(_rk, 4), 120), (512,), 1447, 124967, jnp.int32), jax.random.randint(jax.random.fold_in(jax.random.fold_in(_rk, 4), 121), (512,), 15, 999722, jnp.int32), jax.random.randint(jax.random.fold_in(jax.random.fold_in(_rk, 4), 122), (512,), 1783, 999843, jnp.int32), jax.random.randint(jax.random.fold_in(jax.random.fold_in(_rk, 4), 123), (512,), 792, 999713, jnp.int32), jax.random.randint(jax.random.fold_in(jax.random.fold_in(_rk, 4), 124), (512,), 415, 998043, jnp.int32), jax.random.randint(jax.random.fold_in(jax.random.fold_in(_rk, 4), 125), (512,), 1910, 997998, jnp.int32), jax.random.randint(jax.random.fold_in(jax.random.fold_in(_rk, 4), 126), (512,), 1370, 999233, jnp.int32), jax.random.randint(jax.random.fold_in(jax.random.fold_in(_rk, 4), 127), (512,), 2354, 999182, jnp.int32), jax.random.randint(jax.random.fold_in(jax.random.fold_in(_rk, 4), 128), (512,), 50, 999854, jnp.int32), jax.random.randint(jax.random.fold_in(jax.random.fold_in(_rk, 4), 129), (512,), 346, 999558, jnp.int32), jax.random.randint(jax.random.fold_in(jax.random.fold_in(_rk, 4), 130), (512,), 64, 999919, jnp.int32), jax.random.randint(jax.random.fold_in(jax.random.fold_in(_rk, 4), 131), (512,), 2147, 998516, jnp.int32), jax.random.randint(jax.random.fold_in(jax.random.fold_in(_rk, 4), 132), (512,), 818, 999825, jnp.int32), jax.random.randint(jax.random.fold_in(jax.random.fold_in(_rk, 4), 133), (512,), 1612, 998470, jnp.int32), jax.random.randint(jax.random.fold_in(jax.random.fold_in(_rk, 4), 134), (512,), 137, 993603, jnp.int32), jax.random.randint(jax.random.fold_in(jax.random.fold_in(_rk, 4), 135), (512,), 4, 999516, jnp.int32), jax.random.randint(jax.random.fold_in(jax.random.fold_in(_rk, 4), 136), (512,), 368, 999894, jnp.int32), jax.random.randint(jax.random.fold_in(jax.random.fold_in(_rk, 4), 137), (512,), 1538, 999827, jnp.int32), jax.random.randint(jax.random.fold_in(jax.random.fold_in(_rk, 4), 138), (512,), 1004, 999582, jnp.int32), jax.random.randint(jax.random.fold_in(jax.random.fold_in(_rk, 4), 139), (512,), 844, 124957, jnp.int32), jax.random.randint(jax.random.fold_in(jax.random.fold_in(_rk, 4), 140), (512,), 427, 997674, jnp.int32), jax.random.randint(jax.random.fold_in(jax.random.fold_in(_rk, 4), 141), (512,), 1406, 999517, jnp.int32), jax.random.randint(jax.random.fold_in(jax.random.fold_in(_rk, 4), 142), (512,), 1186, 999454, jnp.int32), jax.random.randint(jax.random.fold_in(jax.random.fold_in(_rk, 4), 143), (512,), 42, 999209, jnp.int32), jax.random.randint(jax.random.fold_in(jax.random.fold_in(_rk, 4), 144), (512,), 1087, 999113, jnp.int32), jax.random.randint(jax.random.fold_in(jax.random.fold_in(_rk, 4), 145), (512,), 289, 997769, jnp.int32), jax.random.randint(jax.random.fold_in(jax.random.fold_in(_rk, 4), 146), (512,), 31, 998929, jnp.int32), jax.random.randint(jax.random.fold_in(jax.random.fold_in(_rk, 4), 147), (512,), 2663, 124938, jnp.int32), jax.random.randint(jax.random.fold_in(jax.random.fold_in(_rk, 4), 148), (512,), 376, 999964, jnp.int32), jax.random.randint(jax.random.fold_in(jax.random.fold_in(_rk, 4), 149), (512,), 2067, 997937, jnp.int32), jax.random.randint(jax.random.fold_in(jax.random.fold_in(_rk, 4), 150), (512,), 185, 999028, jnp.int32), jax.random.randint(jax.random.fold_in(jax.random.fold_in(_rk, 4), 151), (512,), 3541, 996974, jnp.int32), jax.random.randint(jax.random.fold_in(jax.random.fold_in(_rk, 4), 152), (512,), 269, 124870, jnp.int32), jax.random.randint(jax.random.fold_in(jax.random.fold_in(_rk, 4), 153), (512,), 230, 998686, jnp.int32), jax.random.randint(jax.random.fold_in(jax.random.fold_in(_rk, 4), 154), (512,), 192, 999668, jnp.int32), jax.random.randint(jax.random.fold_in(jax.random.fold_in(_rk, 4), 155), (512,), 1157, 999662, jnp.int32), jax.random.randint(jax.random.fold_in(jax.random.fold_in(_rk, 4), 156), (512,), 375, 999531, jnp.int32), jax.random.randint(jax.random.fold_in(jax.random.fold_in(_rk, 4), 157), (512,), 1563, 999361, jnp.int32), jax.random.randint(jax.random.fold_in(jax.random.fold_in(_rk, 4), 158), (512,), 1018, 997572, jnp.int32), jax.random.randint(jax.random.fold_in(jax.random.fold_in(_rk, 4), 159), (512,), 3702, 999694, jnp.int32), jax.random.randint(jax.random.fold_in(jax.random.fold_in(_rk, 4), 160), (512,), 8, 998414, jnp.int32), jax.random.randint(jax.random.fold_in(jax.random.fold_in(_rk, 4), 161), (512,), 165, 999293, jnp.int32), jax.random.randint(jax.random.fold_in(jax.random.fold_in(_rk, 4), 162), (512,), 530, 997990, jnp.int32), jax.random.randint(jax.random.fold_in(jax.random.fold_in(_rk, 4), 163), (512,), 165, 999121, jnp.int32), jax.random.randint(jax.random.fold_in(jax.random.fold_in(_rk, 4), 164), (512,), 624, 999206, jnp.int32), jax.random.randint(jax.random.fold_in(jax.random.fold_in(_rk, 4), 165), (512,), 2163, 999785, jnp.int32), jax.random.randint(jax.random.fold_in(jax.random.fold_in(_rk, 4), 166), (512,), 2, 997513, jnp.int32), jax.random.randint(jax.random.fold_in(jax.random.fold_in(_rk, 4), 167), (512,), 712, 998665, jnp.int32), jax.random.randint(jax.random.fold_in(jax.random.fold_in(_rk, 4), 168), (512,), 19, 124736, jnp.int32), jax.random.randint(jax.random.fold_in(jax.random.fold_in(_rk, 4), 169), (512,), 1555, 997999, jnp.int32), jax.random.randint(jax.random.fold_in(jax.random.fold_in(_rk, 4), 170), (512,), 2186, 999590, jnp.int32), jax.random.randint(jax.random.fold_in(jax.random.fold_in(_rk, 4), 171), (512,), 280, 999979, jnp.int32), jax.random.randint(jax.random.fold_in(jax.random.fold_in(_rk, 4), 172), (512,), 86, 999070, jnp.int32), jax.random.randint(jax.random.fold_in(jax.random.fold_in(_rk, 4), 173), (512,), 1040, 999327, jnp.int32), jax.random.randint(jax.random.fold_in(jax.random.fold_in(_rk, 4), 174), (512,), 398, 998549, jnp.int32), jax.random.randint(jax.random.fold_in(jax.random.fold_in(_rk, 4), 175), (512,), 2543, 998991, jnp.int32), jax.random.randint(jax.random.fold_in(jax.random.fold_in(_rk, 4), 176), (512,), 1447, 997884, jnp.int32), jax.random.randint(jax.random.fold_in(jax.random.fold_in(_rk, 4), 177), (512,), 136, 999211, jnp.int32), jax.random.randint(jax.random.fold_in(jax.random.fold_in(_rk, 4), 178), (512,), 2508, 999990, jnp.int32), jax.random.randint(jax.random.fold_in(jax.random.fold_in(_rk, 4), 179), (512,), 340, 999708, jnp.int32), jax.random.randint(jax.random.fold_in(jax.random.fold_in(_rk, 4), 180), (512,), 748, 999659, jnp.int32), jax.random.randint(jax.random.fold_in(jax.random.fold_in(_rk, 4), 181), (512,), 1397, 999635, jnp.int32), jax.random.randint(jax.random.fold_in(jax.random.fold_in(_rk, 4), 182), (512,), 672, 999545, jnp.int32), jax.random.randint(jax.random.fold_in(jax.random.fold_in(_rk, 4), 183), (512,), 338, 999887, jnp.int32), jax.random.randint(jax.random.fold_in(jax.random.fold_in(_rk, 4), 184), (512,), 40, 999713, jnp.int32), jax.random.randint(jax.random.fold_in(jax.random.fold_in(_rk, 4), 185), (512,), 1232, 999750, jnp.int32), jax.random.randint(jax.random.fold_in(jax.random.fold_in(_rk, 4), 186), (512,), 881, 999829, jnp.int32), jax.random.randint(jax.random.fold_in(jax.random.fold_in(_rk, 4), 187), (512,), 270, 124849, jnp.int32), jax.random.randint(jax.random.fold_in(jax.random.fold_in(_rk, 4), 188), (512,), 222, 998989, jnp.int32), jax.random.randint(jax.random.fold_in(jax.random.fold_in(_rk, 4), 189), (512,), 466, 998378, jnp.int32), jax.random.randint(jax.random.fold_in(jax.random.fold_in(_rk, 4), 190), (512,), 40, 999587, jnp.int32), jax.random.randint(jax.random.fold_in(jax.random.fold_in(_rk, 4), 191), (512,), 202, 997065, jnp.int32), jax.random.randint(jax.random.fold_in(jax.random.fold_in(_rk, 4), 192), (512,), 997, 996999, jnp.int32), jax.random.randint(jax.random.fold_in(jax.random.fold_in(_rk, 4), 193), (512,), 1054, 999839, jnp.int32), jax.random.randint(jax.random.fold_in(jax.random.fold_in(_rk, 4), 194), (512,), 3885, 998420, jnp.int32), jax.random.randint(jax.random.fold_in(jax.random.fold_in(_rk, 4), 195), (512,), 537, 997899, jnp.int32), jax.random.randint(jax.random.fold_in(jax.random.fold_in(_rk, 4), 196), (512,), 458, 996269, jnp.int32), jax.random.randint(jax.random.fold_in(jax.random.fold_in(_rk, 4), 197), (512,), 1860, 124918, jnp.int32), jax.random.randint(jax.random.fold_in(jax.random.fold_in(_rk, 4), 198), (512,), 1428, 998847, jnp.int32), jax.random.randint(jax.random.fold_in(jax.random.fold_in(_rk, 4), 199), (512,), 989, 999674, jnp.int32)], axis=1)
        r_historical_cat = jnp.stack([jax.random.randint(jax.random.fold_in(jax.random.fold_in(_rk, 5), 0), (512,), 0, 1000, jnp.int32), jax.random.randint(jax.random.fold_in(jax.random.fold_in(_rk, 5), 1), (512,), 0, 1000, jnp.int32), jax.random.randint(jax.random.fold_in(jax.random.fold_in(_rk, 5), 2), (512,), 0, 999, jnp.int32), jax.random.randint(jax.random.fold_in(jax.random.fold_in(_rk, 5), 3), (512,), 0, 1000, jnp.int32), jax.random.randint(jax.random.fold_in(jax.random.fold_in(_rk, 5), 4), (512,), 0, 1000, jnp.int32), jax.random.randint(jax.random.fold_in(jax.random.fold_in(_rk, 5), 5), (512,), 2, 1000, jnp.int32), jax.random.randint(jax.random.fold_in(jax.random.fold_in(_rk, 5), 6), (512,), 0, 999, jnp.int32), jax.random.randint(jax.random.fold_in(jax.random.fold_in(_rk, 5), 7), (512,), 0, 999, jnp.int32), jax.random.randint(jax.random.fold_in(jax.random.fold_in(_rk, 5), 8), (512,), 0, 1000, jnp.int32), jax.random.randint(jax.random.fold_in(jax.random.fold_in(_rk, 5), 9), (512,), 0, 1000, jnp.int32), jax.random.randint(jax.random.fold_in(jax.random.fold_in(_rk, 5), 10), (512,), 0, 1000, jnp.int32), jax.random.randint(jax.random.fold_in(jax.random.fold_in(_rk, 5), 11), (512,), 0, 1000, jnp.int32), jax.random.randint(jax.random.fold_in(jax.random.fold_in(_rk, 5), 12), (512,), 0, 999, jnp.int32), jax.random.randint(jax.random.fold_in(jax.random.fold_in(_rk, 5), 13), (512,), 3, 999, jnp.int32), jax.random.randint(jax.random.fold_in(jax.random.fold_in(_rk, 5), 14), (512,), 0, 1000, jnp.int32), jax.random.randint(jax.random.fold_in(jax.random.fold_in(_rk, 5), 15), (512,), 0, 1000, jnp.int32), jax.random.randint(jax.random.fold_in(jax.random.fold_in(_rk, 5), 16), (512,), 1, 1000, jnp.int32), jax.random.randint(jax.random.fold_in(jax.random.fold_in(_rk, 5), 17), (512,), 1, 998, jnp.int32), jax.random.randint(jax.random.fold_in(jax.random.fold_in(_rk, 5), 18), (512,), 1, 999, jnp.int32), jax.random.randint(jax.random.fold_in(jax.random.fold_in(_rk, 5), 19), (512,), 1, 1000, jnp.int32), jax.random.randint(jax.random.fold_in(jax.random.fold_in(_rk, 5), 20), (512,), 0, 998, jnp.int32), jax.random.randint(jax.random.fold_in(jax.random.fold_in(_rk, 5), 21), (512,), 0, 1000, jnp.int32), jax.random.randint(jax.random.fold_in(jax.random.fold_in(_rk, 5), 22), (512,), 0, 1000, jnp.int32), jax.random.randint(jax.random.fold_in(jax.random.fold_in(_rk, 5), 23), (512,), 0, 1000, jnp.int32), jax.random.randint(jax.random.fold_in(jax.random.fold_in(_rk, 5), 24), (512,), 0, 1000, jnp.int32), jax.random.randint(jax.random.fold_in(jax.random.fold_in(_rk, 5), 25), (512,), 1, 1000, jnp.int32), jax.random.randint(jax.random.fold_in(jax.random.fold_in(_rk, 5), 26), (512,), 0, 1000, jnp.int32), jax.random.randint(jax.random.fold_in(jax.random.fold_in(_rk, 5), 27), (512,), 0, 1000, jnp.int32), jax.random.randint(jax.random.fold_in(jax.random.fold_in(_rk, 5), 28), (512,), 0, 999, jnp.int32), jax.random.randint(jax.random.fold_in(jax.random.fold_in(_rk, 5), 29), (512,), 0, 999, jnp.int32), jax.random.randint(jax.random.fold_in(jax.random.fold_in(_rk, 5), 30), (512,), 1, 1000, jnp.int32), jax.random.randint(jax.random.fold_in(jax.random.fold_in(_rk, 5), 31), (512,), 0, 1000, jnp.int32), jax.random.randint(jax.random.fold_in(jax.random.fold_in(_rk, 5), 32), (512,), 0, 1000, jnp.int32), jax.random.randint(jax.random.fold_in(jax.random.fold_in(_rk, 5), 33), (512,), 0, 999, jnp.int32), jax.random.randint(jax.random.fold_in(jax.random.fold_in(_rk, 5), 34), (512,), 0, 1000, jnp.int32), jax.random.randint(jax.random.fold_in(jax.random.fold_in(_rk, 5), 35), (512,), 0, 1000, jnp.int32), jax.random.randint(jax.random.fold_in(jax.random.fold_in(_rk, 5), 36), (512,), 1, 1000, jnp.int32), jax.random.randint(jax.random.fold_in(jax.random.fold_in(_rk, 5), 37), (512,), 0, 1000, jnp.int32), jax.random.randint(jax.random.fold_in(jax.random.fold_in(_rk, 5), 38), (512,), 0, 1000, jnp.int32), jax.random.randint(jax.random.fold_in(jax.random.fold_in(_rk, 5), 39), (512,), 1, 1000, jnp.int32), jax.random.randint(jax.random.fold_in(jax.random.fold_in(_rk, 5), 40), (512,), 0, 998, jnp.int32), jax.random.randint(jax.random.fold_in(jax.random.fold_in(_rk, 5), 41), (512,), 0, 1000, jnp.int32), jax.random.randint(jax.random.fold_in(jax.random.fold_in(_rk, 5), 42), (512,), 0, 1000, jnp.int32), jax.random.randint(jax.random.fold_in(jax.random.fold_in(_rk, 5), 43), (512,), 1, 998, jnp.int32), jax.random.randint(jax.random.fold_in(jax.random.fold_in(_rk, 5), 44), (512,), 0, 998, jnp.int32), jax.random.randint(jax.random.fold_in(jax.random.fold_in(_rk, 5), 45), (512,), 1, 1000, jnp.int32), jax.random.randint(jax.random.fold_in(jax.random.fold_in(_rk, 5), 46), (512,), 0, 1000, jnp.int32), jax.random.randint(jax.random.fold_in(jax.random.fold_in(_rk, 5), 47), (512,), 0, 1000, jnp.int32), jax.random.randint(jax.random.fold_in(jax.random.fold_in(_rk, 5), 48), (512,), 0, 1000, jnp.int32), jax.random.randint(jax.random.fold_in(jax.random.fold_in(_rk, 5), 49), (512,), 1, 1000, jnp.int32), jax.random.randint(jax.random.fold_in(jax.random.fold_in(_rk, 5), 50), (512,), 0, 999, jnp.int32), jax.random.randint(jax.random.fold_in(jax.random.fold_in(_rk, 5), 51), (512,), 0, 998, jnp.int32), jax.random.randint(jax.random.fold_in(jax.random.fold_in(_rk, 5), 52), (512,), 0, 1000, jnp.int32), jax.random.randint(jax.random.fold_in(jax.random.fold_in(_rk, 5), 53), (512,), 0, 1000, jnp.int32), jax.random.randint(jax.random.fold_in(jax.random.fold_in(_rk, 5), 54), (512,), 0, 999, jnp.int32), jax.random.randint(jax.random.fold_in(jax.random.fold_in(_rk, 5), 55), (512,), 1, 996, jnp.int32), jax.random.randint(jax.random.fold_in(jax.random.fold_in(_rk, 5), 56), (512,), 1, 999, jnp.int32), jax.random.randint(jax.random.fold_in(jax.random.fold_in(_rk, 5), 57), (512,), 1, 999, jnp.int32), jax.random.randint(jax.random.fold_in(jax.random.fold_in(_rk, 5), 58), (512,), 0, 1000, jnp.int32), jax.random.randint(jax.random.fold_in(jax.random.fold_in(_rk, 5), 59), (512,), 0, 999, jnp.int32), jax.random.randint(jax.random.fold_in(jax.random.fold_in(_rk, 5), 60), (512,), 1, 1000, jnp.int32), jax.random.randint(jax.random.fold_in(jax.random.fold_in(_rk, 5), 61), (512,), 0, 999, jnp.int32), jax.random.randint(jax.random.fold_in(jax.random.fold_in(_rk, 5), 62), (512,), 0, 999, jnp.int32), jax.random.randint(jax.random.fold_in(jax.random.fold_in(_rk, 5), 63), (512,), 0, 1000, jnp.int32), jax.random.randint(jax.random.fold_in(jax.random.fold_in(_rk, 5), 64), (512,), 0, 1000, jnp.int32), jax.random.randint(jax.random.fold_in(jax.random.fold_in(_rk, 5), 65), (512,), 0, 1000, jnp.int32), jax.random.randint(jax.random.fold_in(jax.random.fold_in(_rk, 5), 66), (512,), 0, 1000, jnp.int32), jax.random.randint(jax.random.fold_in(jax.random.fold_in(_rk, 5), 67), (512,), 1, 998, jnp.int32), jax.random.randint(jax.random.fold_in(jax.random.fold_in(_rk, 5), 68), (512,), 0, 999, jnp.int32), jax.random.randint(jax.random.fold_in(jax.random.fold_in(_rk, 5), 69), (512,), 1, 1000, jnp.int32), jax.random.randint(jax.random.fold_in(jax.random.fold_in(_rk, 5), 70), (512,), 1, 997, jnp.int32), jax.random.randint(jax.random.fold_in(jax.random.fold_in(_rk, 5), 71), (512,), 0, 1000, jnp.int32), jax.random.randint(jax.random.fold_in(jax.random.fold_in(_rk, 5), 72), (512,), 0, 999, jnp.int32), jax.random.randint(jax.random.fold_in(jax.random.fold_in(_rk, 5), 73), (512,), 0, 1000, jnp.int32), jax.random.randint(jax.random.fold_in(jax.random.fold_in(_rk, 5), 74), (512,), 1, 998, jnp.int32), jax.random.randint(jax.random.fold_in(jax.random.fold_in(_rk, 5), 75), (512,), 1, 1000, jnp.int32), jax.random.randint(jax.random.fold_in(jax.random.fold_in(_rk, 5), 76), (512,), 0, 1000, jnp.int32), jax.random.randint(jax.random.fold_in(jax.random.fold_in(_rk, 5), 77), (512,), 0, 1000, jnp.int32), jax.random.randint(jax.random.fold_in(jax.random.fold_in(_rk, 5), 78), (512,), 0, 1000, jnp.int32), jax.random.randint(jax.random.fold_in(jax.random.fold_in(_rk, 5), 79), (512,), 0, 1000, jnp.int32), jax.random.randint(jax.random.fold_in(jax.random.fold_in(_rk, 5), 80), (512,), 0, 1000, jnp.int32), jax.random.randint(jax.random.fold_in(jax.random.fold_in(_rk, 5), 81), (512,), 0, 1000, jnp.int32), jax.random.randint(jax.random.fold_in(jax.random.fold_in(_rk, 5), 82), (512,), 4, 999, jnp.int32), jax.random.randint(jax.random.fold_in(jax.random.fold_in(_rk, 5), 83), (512,), 1, 1000, jnp.int32), jax.random.randint(jax.random.fold_in(jax.random.fold_in(_rk, 5), 84), (512,), 0, 1000, jnp.int32), jax.random.randint(jax.random.fold_in(jax.random.fold_in(_rk, 5), 85), (512,), 0, 996, jnp.int32), jax.random.randint(jax.random.fold_in(jax.random.fold_in(_rk, 5), 86), (512,), 0, 998, jnp.int32), jax.random.randint(jax.random.fold_in(jax.random.fold_in(_rk, 5), 87), (512,), 1, 1000, jnp.int32), jax.random.randint(jax.random.fold_in(jax.random.fold_in(_rk, 5), 88), (512,), 1, 1000, jnp.int32), jax.random.randint(jax.random.fold_in(jax.random.fold_in(_rk, 5), 89), (512,), 0, 999, jnp.int32), jax.random.randint(jax.random.fold_in(jax.random.fold_in(_rk, 5), 90), (512,), 1, 1000, jnp.int32), jax.random.randint(jax.random.fold_in(jax.random.fold_in(_rk, 5), 91), (512,), 1, 999, jnp.int32), jax.random.randint(jax.random.fold_in(jax.random.fold_in(_rk, 5), 92), (512,), 1, 1000, jnp.int32), jax.random.randint(jax.random.fold_in(jax.random.fold_in(_rk, 5), 93), (512,), 0, 1000, jnp.int32), jax.random.randint(jax.random.fold_in(jax.random.fold_in(_rk, 5), 94), (512,), 4, 999, jnp.int32), jax.random.randint(jax.random.fold_in(jax.random.fold_in(_rk, 5), 95), (512,), 0, 1000, jnp.int32), jax.random.randint(jax.random.fold_in(jax.random.fold_in(_rk, 5), 96), (512,), 1, 999, jnp.int32), jax.random.randint(jax.random.fold_in(jax.random.fold_in(_rk, 5), 97), (512,), 0, 999, jnp.int32), jax.random.randint(jax.random.fold_in(jax.random.fold_in(_rk, 5), 98), (512,), 0, 1000, jnp.int32), jax.random.randint(jax.random.fold_in(jax.random.fold_in(_rk, 5), 99), (512,), 3, 1000, jnp.int32), jax.random.randint(jax.random.fold_in(jax.random.fold_in(_rk, 5), 100), (512,), 1, 999, jnp.int32), jax.random.randint(jax.random.fold_in(jax.random.fold_in(_rk, 5), 101), (512,), 2, 1000, jnp.int32), jax.random.randint(jax.random.fold_in(jax.random.fold_in(_rk, 5), 102), (512,), 1, 1000, jnp.int32), jax.random.randint(jax.random.fold_in(jax.random.fold_in(_rk, 5), 103), (512,), 0, 1000, jnp.int32), jax.random.randint(jax.random.fold_in(jax.random.fold_in(_rk, 5), 104), (512,), 1, 1000, jnp.int32), jax.random.randint(jax.random.fold_in(jax.random.fold_in(_rk, 5), 105), (512,), 1, 1000, jnp.int32), jax.random.randint(jax.random.fold_in(jax.random.fold_in(_rk, 5), 106), (512,), 0, 1000, jnp.int32), jax.random.randint(jax.random.fold_in(jax.random.fold_in(_rk, 5), 107), (512,), 2, 998, jnp.int32), jax.random.randint(jax.random.fold_in(jax.random.fold_in(_rk, 5), 108), (512,), 1, 999, jnp.int32), jax.random.randint(jax.random.fold_in(jax.random.fold_in(_rk, 5), 109), (512,), 0, 999, jnp.int32), jax.random.randint(jax.random.fold_in(jax.random.fold_in(_rk, 5), 110), (512,), 0, 1000, jnp.int32), jax.random.randint(jax.random.fold_in(jax.random.fold_in(_rk, 5), 111), (512,), 1, 1000, jnp.int32), jax.random.randint(jax.random.fold_in(jax.random.fold_in(_rk, 5), 112), (512,), 0, 1000, jnp.int32), jax.random.randint(jax.random.fold_in(jax.random.fold_in(_rk, 5), 113), (512,), 0, 1000, jnp.int32), jax.random.randint(jax.random.fold_in(jax.random.fold_in(_rk, 5), 114), (512,), 2, 999, jnp.int32), jax.random.randint(jax.random.fold_in(jax.random.fold_in(_rk, 5), 115), (512,), 0, 999, jnp.int32), jax.random.randint(jax.random.fold_in(jax.random.fold_in(_rk, 5), 116), (512,), 0, 999, jnp.int32), jax.random.randint(jax.random.fold_in(jax.random.fold_in(_rk, 5), 117), (512,), 0, 1000, jnp.int32), jax.random.randint(jax.random.fold_in(jax.random.fold_in(_rk, 5), 118), (512,), 1, 998, jnp.int32), jax.random.randint(jax.random.fold_in(jax.random.fold_in(_rk, 5), 119), (512,), 0, 1000, jnp.int32), jax.random.randint(jax.random.fold_in(jax.random.fold_in(_rk, 5), 120), (512,), 0, 1000, jnp.int32), jax.random.randint(jax.random.fold_in(jax.random.fold_in(_rk, 5), 121), (512,), 0, 1000, jnp.int32), jax.random.randint(jax.random.fold_in(jax.random.fold_in(_rk, 5), 122), (512,), 0, 1000, jnp.int32), jax.random.randint(jax.random.fold_in(jax.random.fold_in(_rk, 5), 123), (512,), 1, 997, jnp.int32), jax.random.randint(jax.random.fold_in(jax.random.fold_in(_rk, 5), 124), (512,), 0, 1000, jnp.int32), jax.random.randint(jax.random.fold_in(jax.random.fold_in(_rk, 5), 125), (512,), 0, 1000, jnp.int32), jax.random.randint(jax.random.fold_in(jax.random.fold_in(_rk, 5), 126), (512,), 0, 1000, jnp.int32), jax.random.randint(jax.random.fold_in(jax.random.fold_in(_rk, 5), 127), (512,), 0, 1000, jnp.int32), jax.random.randint(jax.random.fold_in(jax.random.fold_in(_rk, 5), 128), (512,), 0, 999, jnp.int32), jax.random.randint(jax.random.fold_in(jax.random.fold_in(_rk, 5), 129), (512,), 0, 999, jnp.int32), jax.random.randint(jax.random.fold_in(jax.random.fold_in(_rk, 5), 130), (512,), 0, 999, jnp.int32), jax.random.randint(jax.random.fold_in(jax.random.fold_in(_rk, 5), 131), (512,), 0, 999, jnp.int32), jax.random.randint(jax.random.fold_in(jax.random.fold_in(_rk, 5), 132), (512,), 1, 1000, jnp.int32), jax.random.randint(jax.random.fold_in(jax.random.fold_in(_rk, 5), 133), (512,), 0, 1000, jnp.int32), jax.random.randint(jax.random.fold_in(jax.random.fold_in(_rk, 5), 134), (512,), 1, 1000, jnp.int32), jax.random.randint(jax.random.fold_in(jax.random.fold_in(_rk, 5), 135), (512,), 0, 999, jnp.int32), jax.random.randint(jax.random.fold_in(jax.random.fold_in(_rk, 5), 136), (512,), 0, 999, jnp.int32), jax.random.randint(jax.random.fold_in(jax.random.fold_in(_rk, 5), 137), (512,), 2, 999, jnp.int32), jax.random.randint(jax.random.fold_in(jax.random.fold_in(_rk, 5), 138), (512,), 1, 1000, jnp.int32), jax.random.randint(jax.random.fold_in(jax.random.fold_in(_rk, 5), 139), (512,), 1, 1000, jnp.int32), jax.random.randint(jax.random.fold_in(jax.random.fold_in(_rk, 5), 140), (512,), 0, 1000, jnp.int32), jax.random.randint(jax.random.fold_in(jax.random.fold_in(_rk, 5), 141), (512,), 0, 1000, jnp.int32), jax.random.randint(jax.random.fold_in(jax.random.fold_in(_rk, 5), 142), (512,), 0, 998, jnp.int32), jax.random.randint(jax.random.fold_in(jax.random.fold_in(_rk, 5), 143), (512,), 0, 1000, jnp.int32), jax.random.randint(jax.random.fold_in(jax.random.fold_in(_rk, 5), 144), (512,), 3, 997, jnp.int32), jax.random.randint(jax.random.fold_in(jax.random.fold_in(_rk, 5), 145), (512,), 0, 999, jnp.int32), jax.random.randint(jax.random.fold_in(jax.random.fold_in(_rk, 5), 146), (512,), 0, 999, jnp.int32), jax.random.randint(jax.random.fold_in(jax.random.fold_in(_rk, 5), 147), (512,), 0, 999, jnp.int32), jax.random.randint(jax.random.fold_in(jax.random.fold_in(_rk, 5), 148), (512,), 0, 999, jnp.int32), jax.random.randint(jax.random.fold_in(jax.random.fold_in(_rk, 5), 149), (512,), 0, 1000, jnp.int32), jax.random.randint(jax.random.fold_in(jax.random.fold_in(_rk, 5), 150), (512,), 1, 998, jnp.int32), jax.random.randint(jax.random.fold_in(jax.random.fold_in(_rk, 5), 151), (512,), 0, 1000, jnp.int32), jax.random.randint(jax.random.fold_in(jax.random.fold_in(_rk, 5), 152), (512,), 0, 1000, jnp.int32), jax.random.randint(jax.random.fold_in(jax.random.fold_in(_rk, 5), 153), (512,), 0, 996, jnp.int32), jax.random.randint(jax.random.fold_in(jax.random.fold_in(_rk, 5), 154), (512,), 0, 1000, jnp.int32), jax.random.randint(jax.random.fold_in(jax.random.fold_in(_rk, 5), 155), (512,), 1, 1000, jnp.int32), jax.random.randint(jax.random.fold_in(jax.random.fold_in(_rk, 5), 156), (512,), 0, 997, jnp.int32), jax.random.randint(jax.random.fold_in(jax.random.fold_in(_rk, 5), 157), (512,), 1, 1000, jnp.int32), jax.random.randint(jax.random.fold_in(jax.random.fold_in(_rk, 5), 158), (512,), 0, 998, jnp.int32), jax.random.randint(jax.random.fold_in(jax.random.fold_in(_rk, 5), 159), (512,), 0, 999, jnp.int32), jax.random.randint(jax.random.fold_in(jax.random.fold_in(_rk, 5), 160), (512,), 0, 1000, jnp.int32), jax.random.randint(jax.random.fold_in(jax.random.fold_in(_rk, 5), 161), (512,), 1, 999, jnp.int32), jax.random.randint(jax.random.fold_in(jax.random.fold_in(_rk, 5), 162), (512,), 0, 1000, jnp.int32), jax.random.randint(jax.random.fold_in(jax.random.fold_in(_rk, 5), 163), (512,), 1, 1000, jnp.int32), jax.random.randint(jax.random.fold_in(jax.random.fold_in(_rk, 5), 164), (512,), 0, 1000, jnp.int32), jax.random.randint(jax.random.fold_in(jax.random.fold_in(_rk, 5), 165), (512,), 3, 998, jnp.int32), jax.random.randint(jax.random.fold_in(jax.random.fold_in(_rk, 5), 166), (512,), 0, 1000, jnp.int32), jax.random.randint(jax.random.fold_in(jax.random.fold_in(_rk, 5), 167), (512,), 2, 1000, jnp.int32), jax.random.randint(jax.random.fold_in(jax.random.fold_in(_rk, 5), 168), (512,), 0, 999, jnp.int32), jax.random.randint(jax.random.fold_in(jax.random.fold_in(_rk, 5), 169), (512,), 0, 1000, jnp.int32), jax.random.randint(jax.random.fold_in(jax.random.fold_in(_rk, 5), 170), (512,), 0, 1000, jnp.int32), jax.random.randint(jax.random.fold_in(jax.random.fold_in(_rk, 5), 171), (512,), 2, 1000, jnp.int32), jax.random.randint(jax.random.fold_in(jax.random.fold_in(_rk, 5), 172), (512,), 0, 999, jnp.int32), jax.random.randint(jax.random.fold_in(jax.random.fold_in(_rk, 5), 173), (512,), 1, 1000, jnp.int32), jax.random.randint(jax.random.fold_in(jax.random.fold_in(_rk, 5), 174), (512,), 0, 999, jnp.int32), jax.random.randint(jax.random.fold_in(jax.random.fold_in(_rk, 5), 175), (512,), 0, 1000, jnp.int32), jax.random.randint(jax.random.fold_in(jax.random.fold_in(_rk, 5), 176), (512,), 2, 1000, jnp.int32), jax.random.randint(jax.random.fold_in(jax.random.fold_in(_rk, 5), 177), (512,), 0, 1000, jnp.int32), jax.random.randint(jax.random.fold_in(jax.random.fold_in(_rk, 5), 178), (512,), 0, 1000, jnp.int32), jax.random.randint(jax.random.fold_in(jax.random.fold_in(_rk, 5), 179), (512,), 0, 999, jnp.int32), jax.random.randint(jax.random.fold_in(jax.random.fold_in(_rk, 5), 180), (512,), 0, 1000, jnp.int32), jax.random.randint(jax.random.fold_in(jax.random.fold_in(_rk, 5), 181), (512,), 0, 997, jnp.int32), jax.random.randint(jax.random.fold_in(jax.random.fold_in(_rk, 5), 182), (512,), 0, 997, jnp.int32), jax.random.randint(jax.random.fold_in(jax.random.fold_in(_rk, 5), 183), (512,), 0, 1000, jnp.int32), jax.random.randint(jax.random.fold_in(jax.random.fold_in(_rk, 5), 184), (512,), 0, 1000, jnp.int32), jax.random.randint(jax.random.fold_in(jax.random.fold_in(_rk, 5), 185), (512,), 1, 1000, jnp.int32), jax.random.randint(jax.random.fold_in(jax.random.fold_in(_rk, 5), 186), (512,), 2, 999, jnp.int32), jax.random.randint(jax.random.fold_in(jax.random.fold_in(_rk, 5), 187), (512,), 1, 998, jnp.int32), jax.random.randint(jax.random.fold_in(jax.random.fold_in(_rk, 5), 188), (512,), 0, 1000, jnp.int32), jax.random.randint(jax.random.fold_in(jax.random.fold_in(_rk, 5), 189), (512,), 0, 1000, jnp.int32), jax.random.randint(jax.random.fold_in(jax.random.fold_in(_rk, 5), 190), (512,), 0, 1000, jnp.int32), jax.random.randint(jax.random.fold_in(jax.random.fold_in(_rk, 5), 191), (512,), 0, 999, jnp.int32), jax.random.randint(jax.random.fold_in(jax.random.fold_in(_rk, 5), 192), (512,), 0, 1000, jnp.int32), jax.random.randint(jax.random.fold_in(jax.random.fold_in(_rk, 5), 193), (512,), 1, 1000, jnp.int32), jax.random.randint(jax.random.fold_in(jax.random.fold_in(_rk, 5), 194), (512,), 1, 1000, jnp.int32), jax.random.randint(jax.random.fold_in(jax.random.fold_in(_rk, 5), 195), (512,), 0, 997, jnp.int32), jax.random.randint(jax.random.fold_in(jax.random.fold_in(_rk, 5), 196), (512,), 0, 1000, jnp.int32), jax.random.randint(jax.random.fold_in(jax.random.fold_in(_rk, 5), 197), (512,), 2, 999, jnp.int32), jax.random.randint(jax.random.fold_in(jax.random.fold_in(_rk, 5), 198), (512,), 0, 1000, jnp.int32), jax.random.randint(jax.random.fold_in(jax.random.fold_in(_rk, 5), 199), (512,), 0, 1000, jnp.int32)], axis=1)
        r_mask = jax.random.randint(jax.random.fold_in(_rk, 6), (512, 200), 0, 2, jnp.int32)
        return (r_uid, r_mid, r_cat, r_historical_mid, r_historical_cat, r_mask)
    r_uid, r_mid, r_cat, r_historical_mid, r_historical_cat, r_mask = _rec_inputs()

    def _L0_rec_setup():
        import jax, jax.numpy as jnp
        import numpy as np
        B, T, E = (1024, 200, 64)
        NU, NM, NC = (12500, 125000, 1000)
        D_LAU_IN = 8 * E
        D_MLP_IN = 7 * E
        EPS = 1e-05
        NEG = -2.0 ** 31

        def _bn(x, g, b):
            mu = jnp.mean(x, axis=0)
            var = jnp.var(x, axis=0)
            return (x - mu) * jax.lax.rsqrt(var + EPS) * g + b
        key = jax.random.key(seed)
        ks = jax.random.split(key, 32)
        f = lambda k, shape, s=0.05: jax.random.normal(k, shape, dtype=jnp.float32) * s
        inp = {'uid': jax.random.randint(ks[0], (B,), 0, NU, dtype=jnp.int32), 'mid': jax.random.randint(ks[1], (B,), 0, NM, dtype=jnp.int32), 'cat': jax.random.randint(ks[2], (B,), 0, NC, dtype=jnp.int32), 'historical_mid': jax.random.randint(ks[3], (B, T), 0, NM, dtype=jnp.int32), 'historical_cat': jax.random.randint(ks[4], (B, T), 0, NC, dtype=jnp.int32), 'mask': jax.random.randint(ks[5], (B, T), 0, 2, dtype=jnp.int32), 'user_table': f(ks[6], (NU, E), 0.1), 'mat_table': f(ks[7], (NM, E), 0.1), 'cat_table': f(ks[8], (NC, E), 0.1), 'lau_w1': f(ks[9], (D_LAU_IN, 256)), 'lau_b1': f(ks[10], (256,)), 'lau_w2': f(ks[11], (256, 128)), 'lau_b2': f(ks[12], (128,)), 'lau_w3': f(ks[13], (128, 1)), 'lau_b3': f(ks[14], (1,)), 'bn0_g': jnp.ones((D_MLP_IN,), jnp.float32), 'bn0_b': jnp.zeros((D_MLP_IN,), jnp.float32), 'mlp_w1': f(ks[15], (D_MLP_IN, 512)), 'mlp_b1': f(ks[16], (512,)), 'bn1_g': jnp.ones((512,), jnp.float32), 'bn1_b': jnp.zeros((512,), jnp.float32), 'mlp_w2': f(ks[17], (512, 256)), 'mlp_b2': f(ks[18], (256,)), 'bn2_g': jnp.ones((256,), jnp.float32), 'bn2_b': jnp.zeros((256,), jnp.float32), 'mlp_w3': f(ks[19], (256, 2)), 'mlp_b3': f(ks[20], (2,))}
        return inp
    _L0_rec_all = _L0_rec_setup()
    _L0_rec_in = {k: v for k, v in _L0_rec_all.items() if k in ('user_table', 'mat_table', 'cat_table', 'lau_w1', 'lau_b1', 'lau_w2', 'lau_b2', 'lau_w3', 'lau_b3', 'bn0_g', 'bn0_b', 'mlp_w1', 'mlp_b1', 'bn1_g', 'bn1_b', 'mlp_w2', 'mlp_b2', 'bn2_g', 'bn2_b', 'mlp_w3', 'mlp_b3')}
    del _L0_rec_all
    return {'r_uid': r_uid, 'r_mid': r_mid, 'r_cat': r_cat, 'r_historical_mid': r_historical_mid, 'r_historical_cat': r_historical_cat, 'r_mask': r_mask, 'L0_rec_user_table': _L0_rec_in['user_table'], 'L0_rec_mat_table': _L0_rec_in['mat_table'], 'L0_rec_cat_table': _L0_rec_in['cat_table'], 'L0_rec_lau_w1': _L0_rec_in['lau_w1'], 'L0_rec_lau_b1': _L0_rec_in['lau_b1'], 'L0_rec_lau_w2': _L0_rec_in['lau_w2'], 'L0_rec_lau_b2': _L0_rec_in['lau_b2'], 'L0_rec_lau_w3': _L0_rec_in['lau_w3'], 'L0_rec_lau_b3': _L0_rec_in['lau_b3'], 'L0_rec_bn0_g': _L0_rec_in['bn0_g'], 'L0_rec_bn0_b': _L0_rec_in['bn0_b'], 'L0_rec_mlp_w1': _L0_rec_in['mlp_w1'], 'L0_rec_mlp_b1': _L0_rec_in['mlp_b1'], 'L0_rec_bn1_g': _L0_rec_in['bn1_g'], 'L0_rec_bn1_b': _L0_rec_in['bn1_b'], 'L0_rec_mlp_w2': _L0_rec_in['mlp_w2'], 'L0_rec_mlp_b2': _L0_rec_in['mlp_b2'], 'L0_rec_bn2_g': _L0_rec_in['bn2_g'], 'L0_rec_bn2_b': _L0_rec_in['bn2_b'], 'L0_rec_mlp_w3': _L0_rec_in['mlp_w3'], 'L0_rec_mlp_b3': _L0_rec_in['mlp_b3']}

def reference(r_uid, r_mid, r_cat, r_historical_mid, r_historical_cat, r_mask, L0_rec_user_table, L0_rec_mat_table, L0_rec_cat_table, L0_rec_lau_w1, L0_rec_lau_b1, L0_rec_lau_w2, L0_rec_lau_b2, L0_rec_lau_w3, L0_rec_lau_b3, L0_rec_bn0_g, L0_rec_bn0_b, L0_rec_mlp_w1, L0_rec_mlp_b1, L0_rec_bn1_g, L0_rec_bn1_b, L0_rec_mlp_w2, L0_rec_mlp_b2, L0_rec_bn2_g, L0_rec_bn2_b, L0_rec_mlp_w3, L0_rec_mlp_b3):
    import jax
    import jax.numpy as jnp

    def _L0_rec_ref(uid, mid, cat, historical_mid, historical_cat, mask, user_table, mat_table, cat_table, lau_w1, lau_b1, lau_w2, lau_b2, lau_w3, lau_b3, bn0_g, bn0_b, mlp_w1, mlp_b1, bn1_g, bn1_b, mlp_w2, mlp_b2, bn2_g, bn2_b, mlp_w3, mlp_b3):
        import jax, jax.numpy as jnp
        import numpy as np
        B, T, E = (1024, 200, 64)
        NU, NM, NC = (12500, 125000, 1000)
        D_LAU_IN = 8 * E
        D_MLP_IN = 7 * E
        EPS = 1e-05
        NEG = -2.0 ** 31

        def _bn(x, g, b):
            mu = jnp.mean(x, axis=0)
            var = jnp.var(x, axis=0)
            return (x - mu) * jax.lax.rsqrt(var + EPS) * g + b
        u = user_table[uid]
        cur = jnp.concatenate([mat_table[mid], cat_table[cat]], axis=1)
        hist = jnp.concatenate([mat_table[historical_mid], cat_table[historical_cat]], axis=2)
        maskf = mask.astype(hist.dtype)
        cur_e = jnp.broadcast_to(cur[:, None, :], hist.shape)
        comb = jnp.concatenate([cur_e, hist, cur_e - hist, cur_e * hist], axis=2)
        h = jax.nn.sigmoid(comb @ lau_w1 + lau_b1)
        h = jax.nn.sigmoid(h @ lau_w2 + lau_b2)
        aw = (h @ lau_w3 + lau_b3)[..., 0]
        masked = jnp.where(mask == 1, aw, jnp.asarray(NEG, aw.dtype))
        scores = jax.nn.softmax(masked, axis=-1) * maskf
        lau = jnp.einsum('bt,bte->be', scores, hist)
        hsum = jnp.einsum('bt,bte->be', maskf, hist)
        hmean = hsum / jnp.sum(maskf, axis=1, keepdims=True)
        x = jnp.concatenate([u, cur, lau, hmean], axis=-1)
        x = _bn(x, bn0_g, bn0_b)
        x = jax.nn.leaky_relu(_bn(x @ mlp_w1 + mlp_b1, bn1_g, bn1_b), 0.1)
        x = jax.nn.leaky_relu(_bn(x @ mlp_w2 + mlp_b2, bn2_g, bn2_b), 0.1)
        return x @ mlp_w3 + mlp_b3
    y = _L0_rec_ref(r_uid, r_mid, r_cat, r_historical_mid, r_historical_cat, r_mask, L0_rec_user_table, L0_rec_mat_table, L0_rec_cat_table, L0_rec_lau_w1, L0_rec_lau_b1, L0_rec_lau_w2, L0_rec_lau_b2, L0_rec_lau_w3, L0_rec_lau_b3, L0_rec_bn0_g, L0_rec_bn0_b, L0_rec_mlp_w1, L0_rec_mlp_b1, L0_rec_bn1_g, L0_rec_bn1_b, L0_rec_mlp_w2, L0_rec_mlp_b2, L0_rec_bn2_g, L0_rec_bn2_b, L0_rec_mlp_w3, L0_rec_mlp_b3)
    return y

_drawn_inputs = setup_inputs


def setup_inputs(seed=0):
    import zlib

    import numpy as np

    out = dict(_drawn_inputs(seed))
    spreads = {'L0_rec_bn0_g': (1.0, 0.2),
     'L0_rec_bn0_b': (0.0, 0.8),
     'L0_rec_bn1_g': (1.0, 0.2),
     'L0_rec_bn1_b': (0.0, 0.1),
     'L0_rec_bn2_g': (1.0, 0.2),
     'L0_rec_bn2_b': (0.0, 0.1)}
    factors = {'L0_rec_lau_w1': 8.0,
     'L0_rec_lau_b1': 8.0,
     'L0_rec_lau_w2': 8.0,
     'L0_rec_lau_b2': 8.0,
     'L0_rec_lau_w3': 8.0,
     'L0_rec_mlp_b1': 8.0,
     'L0_rec_mlp_b2': 8.0}
    for name, (base, spread) in spreads.items():
        noise = np.random.default_rng([zlib.crc32(name.encode()), seed]).standard_normal(out[name].shape)
        drawn = base * np.exp(spread * noise) if base else spread * noise
        out[name] = jnp.asarray(drawn.astype(out[name].dtype))
    for name, factor in factors.items():
        out[name] = (out[name] * factor).astype(out[name].dtype)
    return out
```

```python
from contextlib import ExitStack

import concourse.bass as bass
from concourse import mybir

F32 = mybir.dt.float32
I32 = mybir.dt.int32
ALU = mybir.AluOpType
ACT = mybir.ActivationFunctionType
AX = mybir.AxisListType

P = 128
B, T, E = 512, 200, 64
D = 2 * E
C = B // P
H1, H2 = 256, 128
M1 = H1 // P
HALVES = 2
SLOTS = HALVES * P
TILES = 4
COLS = TILES * P
BODY = 8
LAG = 4
F1, F2, NOUT = 512, 256, 2
EPS = 1e-5
NEG = -2.0 ** 31
CHUNKS = [(0, E), (E, D), (E + D, D), (E + 2 * D, D)]


def rec_kernel(nc, r_uid, r_mid, r_cat, r_historical_mid, r_historical_cat, r_mask, user_table,
               mat_table, cat_table, lau_w1, lau_b1, lau_w2, lau_b2, lau_w3, lau_b3, bn0_g, bn0_b,
               mlp_w1, mlp_b1, bn1_g, bn1_b, mlp_w2, mlp_b2, bn2_g, bn2_b, mlp_w3, mlp_b3, out):
    NU, NM, NC = user_table.shape[0], mat_table.shape[0], cat_table.shape[0]
    ctx = ExitStack()
    with ctx:
        ctx.enter_context(nc.allow_non_contiguous_dma(reason="small vectors of parameters"))

        def sb(name, shape, dt=F32):
            return ctx.enter_context(nc.sbuf_tensor(name, shape, dt))

        def bank(name):
            return ctx.enter_context(nc.psum_tensor(name, [P, 512], F32))

        def sem(name):
            return ctx.enter_context(nc.semaphore(name))

        ident = sb("ident", [P, P])
        ones = sb("ones", [P, P])
        w1_raw = sb("w1_raw", [P, 4, H1])
        w_base = sb("w_base", [P, H1])
        w_cur = sb("w_cur", [P, H1])
        w_prod = w1_raw[:, 3, :]
        b1_col = sb("b1_col", [P, M1])
        b1_half = sb("b1_half", [P, M1])
        w2_sb = sb("w2_sb", [P, M1, H2])
        b2_col = sb("b2_col", [P, 1])
        b2_half = sb("b2_half", [P, 1])
        z2_bias = sb("z2_bias", [P, 1])
        w3_sb = sb("w3_sb", [P, 1])
        w3_wide = sb("w3_wide", [P, P])
        b3_all = sb("b3_all", [P, 1])
        score_bias = sb("score_bias", [P, 1])
        bn0 = sb("bn0", [P, 2, 4])
        bn1 = sb("bn1", [P, 2, 4])
        bn2 = sb("bn2", [P, 2, 2])
        mw1 = sb("mw1", [P, 4, F1])
        mb1 = sb("mb1", [P, 4])
        mw2 = sb("mw2", [P, 4, F2])
        mb2 = sb("mb2", [P, 2])
        mw3 = sb("mw3", [P, 2, NOUT])
        mb3 = sb("mb3", [P, NOUT])

        own_raw = sb("own_raw", [P, 3, C], I32)
        own_wrap = sb("own_wrap", [P, 3, C])
        own_sum = sb("own_sum", [P, 3, C])
        own_idx = sb("own_idx", [P, 3, C], I32)
        tok_raw = sb("tok_raw", [P, 3, C, T], I32)
        tok_wrap = sb("tok_wrap", [P, 2, C, T])
        tok_sum = sb("tok_sum", [P, 2, C, T])
        tok = sb("tok", [P, 3, C, SLOTS])
        slot_idx = sb("slot_idx", [P, 2, HALVES, B], I32)
        slot_mask = sb("slot_mask", [P, HALVES, B])
        addend = sb("addend", [P, HALVES, B])
        addend_neg = sb("addend_neg", [P, HALVES, B])

        own_tok = sb("own_tok", [P, C, D])
        user_tok = sb("user_tok", [P, C, E])
        cur_t = sb("cur_t", [P, B])
        user_t = sb("user_t", [P, B])
        z1_bias = sb("z1_bias", [P, M1, B])

        idx_ring = sb("idx_ring", [P, BODY, 2, TILES], I32)
        hist = sb("hist", [P, BODY, TILES, D])
        hist_t = sb("hist_t", [P, 2, COLS])
        w_row = sb("w_row", [P, 2, TILES, H1])
        t1 = sb("t1", [P, 2, M1, COLS])
        t2 = sb("t2", [P, 2, COLS])
        masked = sb("masked", [P, TILES])
        neg_max = sb("neg_max", [TILES, 1])
        exps = sb("exps", [TILES, SLOTS])
        exp_sum = sb("exp_sum", [TILES, 1])
        inv_sum = sb("inv_sum", [TILES, 1])
        probs = sb("probs", [TILES, SLOTS])
        pool_w = sb("pool_w", [P, TILES, 2])
        pooled_t = sb("pooled_t", [P, 2, B])

        inv_count = sb("inv_count", [P, B])
        mean_t = sb("mean_t", [P, B])
        x0 = sb("x0", [P, 4, B])
        y1 = sb("y1", [P, 4, B])
        y1n = sb("y1n", [P, 4, B])
        x1 = sb("x1", [P, 4, B])
        y2 = sb("y2", [P, 2, B])
        y2n = sb("y2n", [P, 2, B])
        x2 = sb("x2", [P, 2, B])
        bn_raw = sb("bn_raw", [P, 10, 6])
        bn_mv = sb("bn_mv", [P, 10, 2])
        bn_eps = sb("bn_eps", [P, 10])
        bn_std = sb("bn_std", [P, 10])
        bn_inv = sb("bn_inv", [P, 10])
        bn_scale = sb("bn_scale", [P, 10])
        bn_ms = sb("bn_ms", [P, 10])
        bn_shift = sb("bn_shift", [P, 10])
        result = sb("result", [P, C, NOUT])

        ps_hist = bank("ps_hist")
        ps_z1 = [[bank(f"ps_z1_{k}_{m}") for m in range(M1)] for k in range(2)]
        ps_z2 = bank("ps_z2")
        ps_soft = bank("ps_soft")
        ps_pool = bank("ps_pool")

        loaded_own = sem("loaded_own")
        loaded_tok = sem("loaded_tok")
        loaded_lau = sem("loaded_lau")
        loaded_mlp = sem("loaded_mlp")
        consts_ready = sem("consts_ready")
        own_idx_ready = sem("own_idx_ready")
        own_gathered = sem("own_gathered")
        user_gathered = sem("user_gathered")
        vec = sem("vec")
        tok_ready = sem("tok_ready")
        flipped = sem("flipped")
        taken = sem("taken")
        setup_done = sem("setup_done")
        params_ready = sem("params_ready")

        idx_copied = sem("idx_copied")
        gathered = [sem(f"gathered{k}") for k in range(BODY)]
        hist_flipped = sem("hist_flipped")
        hist_taken = sem("hist_taken")
        w_row_ready = sem("w_row_ready")
        z1_done = sem("z1_done")
        t1_ready = sem("t1_ready")
        z2_done = sem("z2_done")
        t2_ready = sem("t2_ready")
        scores_done = sem("scores_done")
        masked_ready = sem("masked_ready")
        rows_done = sem("rows_done")
        max_ready = sem("max_ready")
        exps_ready = sem("exps_ready")
        inv_ready = sem("inv_ready")
        probs_ready = sem("probs_ready")
        probs_flipped = sem("probs_flipped")
        pool_w_ready = sem("pool_w_ready")
        pooled = sem("pooled")
        pooled_taken = sem("pooled_taken")

        eps_ready = sem("eps_ready")
        std_ready = sem("std_ready")
        x_ready = sem("x_ready")
        mlp_done = sem("mlp_done")
        mlp_taken = sem("mlp_taken")
        stored = sem("stored")

        block = ctx.enter_context(nc.Block())

        def walk(eng, steps, tick, lag=LAG):
            for t in range(BODY):
                tick(t, t)
            with eng.Fori(1, steps // BODY) as i:
                for j in range(BODY):
                    tick(i * BODY + j, j)
            for t in range(steps, steps + lag):
                tick(t, t % BODY)

        def wait(eng, semaphore, count):
            if not isinstance(count, int) or count > 0:
                eng.wait_ge(semaphore, count)

        def there(n, steps):
            return not isinstance(n, int) or 0 <= n < steps

        @block.sync
        def _(sp):
            for k, src in enumerate((r_uid, r_mid, r_cat)):
                sp.dma_start(own_raw[:, k, :], src.rearrange("(p c) -> p c", c=C)).then_inc(loaded_own, 16)
            for k, src in enumerate((r_mask, r_historical_mid, r_historical_cat)):
                sp.dma_start(tok_raw[:, (2, 0, 1)[k], :, :],
                             src.rearrange("(p c) t -> p c t", c=C)).then_inc(loaded_tok, 16)
            sp.dma_start(w1_raw[:, :, :], lau_w1.rearrange("(k p) n -> p k n", p=P)).then_inc(loaded_lau, 16)
            sp.dma_start(b1_col[:, :], lau_b1.rearrange("(m p) -> p m", p=P)).then_inc(loaded_lau, 16)
            sp.dma_start(w2_sb[:, :, :], lau_w2.rearrange("(k p) n -> p k n", p=P)).then_inc(loaded_lau, 16)
            sp.dma_start(b2_col[:, :], lau_b2.rearrange("(p a) -> p a", a=1)).then_inc(loaded_lau, 16)
            sp.dma_start(w3_sb[:, :], lau_w3).then_inc(loaded_lau, 16)
            sp.dma_start(b3_all[:, :], lau_b3.rearrange("(a n) -> a n", a=1).broadcast_to([P, 1])).then_inc(loaded_lau, 16)
            for k, src in enumerate((bn0_g, bn0_b)):
                sp.dma_start(bn0[0:E, k, 0:1], src[0:E].rearrange("(p a) -> p a", a=1)).then_inc(loaded_mlp, 16)
                sp.dma_start(bn0[:, k, 1:4], src[E:].rearrange("(c p) -> p c", p=P)).then_inc(loaded_mlp, 16)
            for k, (g1, g2) in enumerate(((bn1_g, bn2_g), (bn1_b, bn2_b))):
                sp.dma_start(bn1[:, k, :], g1.rearrange("(c p) -> p c", p=P)).then_inc(loaded_mlp, 16)
                sp.dma_start(bn2[:, k, :], g2.rearrange("(c p) -> p c", p=P)).then_inc(loaded_mlp, 16)
            sp.dma_start(mw1[0:E, 0, :], mlp_w1[0:E, :]).then_inc(loaded_mlp, 16)
            sp.dma_start(mw1[:, 1:4, :], mlp_w1[E:, :].rearrange("(c p) n -> p c n", p=P)).then_inc(loaded_mlp, 16)
            sp.dma_start(mb1[:, :], mlp_b1.rearrange("(m p) -> p m", p=P)).then_inc(loaded_mlp, 16)
            sp.dma_start(mw2[:, :, :], mlp_w2.rearrange("(k p) n -> p k n", p=P)).then_inc(loaded_mlp, 16)
            sp.dma_start(mb2[:, :], mlp_b2.rearrange("(m p) -> p m", p=P)).then_inc(loaded_mlp, 16)
            sp.dma_start(mw3[:, :, :], mlp_w3.rearrange("(k p) n -> p k n", p=P)).then_inc(loaded_mlp, 16)
            sp.dma_start(mb3[:, :], mlp_b3.rearrange("(a n) -> a n", a=1).broadcast_to([P, NOUT])).then_inc(loaded_mlp, 16)
            sp.wait_ge(x_ready, 4)
            sp.dma_start(out.rearrange("(c p) n -> p c n", p=P), result[:, :, :]).then_inc(stored, 16)
            sp.wait_ge(stored, 16)
        LOADED_MLP = 16 * 15

        def gather(pool, dst, table, idx, done):
            pool.indirect_dma_start(dst, None, table[:, :],
                                    bass.IndirectOffsetOnAxis(idx, axis=0)).then_inc(done, 16)

        def gather_loop(pool, tpr):
            rows = TILES // tpr
            steps = B // rows

            def copy_idx(n, slot):
                view = idx_ring[:, slot, :, :].rearrange("p k (h r) -> p k h r", h=tpr)
                pool.tensor_copy(view, slot_idx[:, :, 0:tpr, bass.ds(n * rows, rows)]).then_inc(idx_copied, 1)

            def tick(n, slot):
                if not there(n, steps):
                    return
                wait(pool, pooled, n - BODY + 1)
                wait(pool, idx_copied, n + 1)
                if not isinstance(n, int) or n + 1 < steps:
                    after = (slot + 1) % BODY
                    if isinstance(n, int):
                        wait(pool, gathered[after], 128 * ((n + 1) // BODY))
                    else:
                        wait(pool, gathered[after], (n - slot) * 16 + 128 * ((slot + 1) // BODY))
                    copy_idx(n + 1, after)
                for u in range(TILES):
                    r, h = divmod(u, tpr)
                    at = h * rows + r
                    gather(pool, hist[:, slot, u, 0:E], mat_table, idx_ring[:, slot, 0, at:at + 1], gathered[slot])
                    gather(pool, hist[:, slot, u, E:D], cat_table, idx_ring[:, slot, 1, at:at + 1], gathered[slot])

            pool.wait_ge(taken, 3 * HALVES)
            copy_idx(0, 0)
            for t in range(BODY):
                tick(t, t)
            with pool.Fori(1, steps // BODY - 1) as i:
                for j in range(BODY):
                    tick(i * BODY + j, j)
            for t in range(steps - BODY, steps):
                tick(t, t % BODY)

        @block.gpsimd
        def _(pool):
            pool.memset(ident[:, :], 0.0).then_inc(consts_ready, 1)
            pool.memset(ones[:, :], 1.0).then_inc(consts_ready, 1)
            pool.memset(tok[:, :, :, T:SLOTS], 0.0).then_inc(consts_ready, 1)
            pool.wait_ge(consts_ready, 3)
            pool.affine_select(out=ident[:, :], in_=ident[:, :], compare_op=ALU.not_equal, fill=1.0,
                               base=0, pattern=[[-1, P]], channel_multiplier=1).then_inc(consts_ready, 1)
            pool.wait_ge(own_idx_ready, 3)
            for c in range(C):
                gather(pool, own_tok[:, c, 0:E], mat_table, own_idx[:, 1, c:c + 1], own_gathered)
                gather(pool, own_tok[:, c, E:D], cat_table, own_idx[:, 2, c:c + 1], own_gathered)
            gather_loop(pool, HALVES)
            for c in range(C):
                gather(pool, user_tok[:, c, :], user_table, own_idx[:, 0, c:c + 1], user_gathered)

        def tensor_loop(pe, tpr):
            rows = TILES // tpr
            width = tpr * P
            steps = B // rows
            score_cols = ps_soft[:, 0:TILES]
            prob_cols = ps_pool[:, 8:8 + TILES]
            row_major = ps_soft[0:rows, 256:256 + width]

            def tick(t, j):
                n, k = t - 1, (j - 1) % 2
                if there(n, steps):
                    wait(pe, hist_taken, n + 1)
                    wait(pe, w_row_ready, n + 1)
                    wait(pe, t1_ready, M1 * (n - 1))
                    for m in range(M1):
                        for r in range(rows):
                            last = pe.matmul(ps_z1[k][m][:, r * width:(r + 1) * width],
                                             w_row[:, k, r, m * P:(m + 1) * P],
                                             hist_t[:, k, r * width:(r + 1) * width], start=True, stop=True)
                        last.then_inc(z1_done, 1)
                n = t - 4
                if there(n, steps):
                    wait(pe, probs_ready, n + 1)
                    wait(pe, pooled_taken, n)
                    pe.nop(nofuse=True)
                    for h in range(tpr):
                        last = pe.transpose(prob_cols[:, h * rows:(h + 1) * rows],
                                            probs[0:rows, h * P:(h + 1) * P], ident[0:rows, 0:rows])
                    last.then_inc(probs_flipped, 1)
                n, k = t - 3, (j - 3) % 2
                if there(n, steps):
                    wait(pe, t2_ready, n + 1)
                    wait(pe, exps_ready, n)
                    for u in range(TILES):
                        r, h = divmod(u, tpr)
                        at = h * rows + r
                        last = pe.matmul(score_cols[:, at:at + 1], t2[:, k, u * P:(u + 1) * P], w3_sb[:, :],
                                         start=True, stop=True)
                    last.then_inc(scores_done, 1)
                n = t
                if there(n, steps):
                    wait(pe, gathered[j], 128 * (n // BODY + 1) if isinstance(n, int) else (n - j) * 16 + 128)
                    wait(pe, hist_taken, n)
                    for u in range(TILES):
                        last = pe.transpose(ps_hist[:, u * P:(u + 1) * P], hist[:, j, u, :], ident[:, :])
                    last.then_inc(hist_flipped, 1)
                n, k = t - 2, (j - 2) % 2
                if there(n, steps):
                    wait(pe, t1_ready, M1 * (n + 1))
                    wait(pe, t2_ready, n)
                    for m in range(M1):
                        last = pe.matmul(ps_z2[:, :], w2_sb[:, m, :], t1[:, k, m, :],
                                         start=(m == 0), stop=(m == M1 - 1))
                    last.then_inc(z2_done, 1)
                n = t - 3
                if there(n, steps):
                    wait(pe, masked_ready, n + 1)
                    for h in range(tpr):
                        last = pe.transpose(row_major[:, h * P:(h + 1) * P],
                                            masked[:, h * rows:(h + 1) * rows], ident[:, :])
                    last.then_inc(rows_done, 1)
                n, slot = t - 4, (j - 4) % BODY
                if there(n, steps):
                    wait(pe, pool_w_ready, n + 1)
                    for r in range(rows):
                        for h in range(tpr):
                            last = pe.matmul(ps_pool[:, 2 * r:2 * r + 2], hist[:, slot, r * tpr + h, :],
                                             pool_w[:, h * rows + r, :], start=(h == 0), stop=(h == tpr - 1))
                    last.then_inc(pooled, 1)

            walk(pe, steps, tick)

        @block.tensor
        def _(pe):
            pe.wait_ge(consts_ready, 4)
            for k in range(3):
                pe.wait_ge(tok_ready, k + 1)
                for h in range(HALVES):
                    if 2 * k + h >= 2:
                        pe.wait_ge(taken, 2 * k + h - 1)
                    for c in range(C):
                        last = pe.transpose(ps_z1[0][h][:, c * P:(c + 1) * P],
                                            tok[:, (2, 0, 1)[k], c, h * P:(h + 1) * P], ident[:, :])
                    last.then_inc(flipped, 1)
            pe.wait_ge(loaded_lau, 96)
            pe.wait_ge(params_ready, 1)
            for m in range(M1):
                pe.matmul(ps_z2[:, 0:1], w2_sb[:, m, :], ones[:, 0:1], start=(m == 0), stop=(m == M1 - 1))
            pe.matmul(ps_z2[:, 1:2], w3_wide[:, :], ones[:, 0:1], start=True, stop=True).then_inc(flipped, 1)
            pe.wait_ge(own_gathered, 16 * 2 * C)
            for c in range(C):
                last = pe.transpose(ps_hist[:, c * P:(c + 1) * P], own_tok[:, c, :], ident[:, :])
            last.then_inc(flipped, 1)
            pe.wait_ge(taken, 7)
            pe.wait_ge(params_ready, 2)
            for m in range(M1):
                last = pe.matmul(ps_z1[1][m][:, :], w_cur[:, m * P:(m + 1) * P], cur_t[:, :], start=True, stop=True)
                last.then_inc(flipped, 1)
            pe.wait_ge(setup_done, M1)
            tensor_loop(pe, HALVES)
            for h in range(HALVES):
                last = pe.matmul(ps_hist[:, :], ones[:, :], slot_mask[:, h, :], start=(h == 0), stop=(h == HALVES - 1))
            last.then_inc(mlp_done, 1)
            pe.wait_ge(user_gathered, 16 * C)
            for c in range(C):
                last = pe.transpose(ps_z2[0:E, c * P:(c + 1) * P], user_tok[:, c, :], ident[:, :])
            last.then_inc(mlp_done, 1)
            pe.wait_ge(x_ready, 1)
            pe.wait_ge(loaded_mlp, LOADED_MLP)
            for m in range(4):
                for k, (_, size) in enumerate(CHUNKS):
                    last = pe.matmul(ps_z1[m // 2][m % 2][:, :], mw1[0:size, k, m * P:(m + 1) * P],
                                     x0[0:size, k, :], start=(k == 0), stop=(k == 3))
                last.then_inc(mlp_done, 1)
            pe.wait_ge(x_ready, 2)
            for m in range(2):
                for k in range(4):
                    last = pe.matmul((ps_z2, ps_hist)[m][:, :], mw2[:, k, m * P:(m + 1) * P], x1[:, k, :],
                                     start=(k == 0), stop=(k == 3))
                last.then_inc(mlp_done, 1)
            pe.wait_ge(x_ready, 3)
            for c in range(C):
                for k in range(2):
                    last = pe.matmul(ps_pool[:, c * NOUT:(c + 1) * NOUT], x2[:, k, c * P:(c + 1) * P], mw3[:, k, :],
                                     start=(k == 0), stop=(k == 1))
            last.then_inc(mlp_done, 1)

        def scalar_loop(act, tpr):
            rows = TILES // tpr
            width = tpr * P
            steps = B // rows

            def tick(t, j):
                n, k = t - 1, (j - 1) % 2
                if there(n, steps):
                    wait(act, z2_done, n - 1)
                    for m in range(M1):
                        wait(act, z1_done, M1 * n + m + 1)
                        for r in range(rows):
                            last = act.activation(t1[:, k, m, r * width:(r + 1) * width],
                                                  ps_z1[k][m][:, r * width:(r + 1) * width], ACT.Tanh,
                                                  bias=z1_bias[:, m, bass.ds(n * rows + r, 1)], scale=0.5)
                        last.then_inc(t1_ready, 1)
                n, k = t - 2, (j - 2) % 2
                if there(n, steps):
                    wait(act, z2_done, n + 1)
                    wait(act, scores_done, n - 1)
                    act.activation(t2[:, k, :], ps_z2[:, :], ACT.Tanh, bias=z2_bias[:, :],
                                   scale=0.25).then_inc(t2_ready, 1)
                n = t - 3
                if there(n, steps):
                    wait(act, max_ready, n + 1)
                    wait(act, probs_ready, n)
                    act.activation(exps[0:rows, 0:width], ps_soft[0:rows, 256:256 + width], ACT.Exp,
                                   bias=neg_max[0:rows, :], accum_out=exp_sum[0:rows, :]).then_inc(exps_ready, 1)

            walk(act, steps, tick)

        @block.scalar
        def _(act):
            act.wait_ge(setup_done, M1)
            scalar_loop(act, HALVES)

            def std(first, count, need):
                act.wait_ge(eps_ready, need)
                act.activation(bn_std[:, first:first + count], bn_eps[:, first:first + count],
                               ACT.Sqrt).then_inc(std_ready, 1)

            std(0, 4, 1)
            for m in range(4):
                act.wait_ge(mlp_done, 3 + m)
                act.activation(y1[:, m, :], ps_z1[m // 2][m % 2][:, :], ACT.Identity,
                               bias=mb1[:, m:m + 1]).then_inc(mlp_taken, 1)
            std(4, 4, 2)
            for m in range(2):
                act.wait_ge(mlp_done, 7 + m)
                act.activation(y2[:, m, :], (ps_z2, ps_hist)[m][:, :], ACT.Identity,
                               bias=mb2[:, m:m + 1]).then_inc(mlp_taken, 1)
            std(8, 2, 3)

        def vector_loop(dve, tpr):
            rows = TILES // tpr
            width = tpr * P
            steps = B // rows

            def tick(t, j):
                n, k = t, j % 2
                if there(n, steps):
                    wait(dve, z1_done, M1 * (n - 1))
                    for r in range(rows):
                        last = dve.scalar_tensor_tensor(out=w_row[:, k, r, :], in0=w_prod,
                                                        scalar=cur_t[:, bass.ds(n * rows + r, 1)],
                                                        in1=w_base[:, :], op0=ALU.mult, op1=ALU.add)
                    last.then_inc(w_row_ready, 1)
                n = t - 4
                if there(n, steps):
                    wait(dve, probs_flipped, n + 1)
                    wait(dve, pooled, n)
                    mask = slot_mask[:, 0:tpr, bass.ds(n * rows, rows)]
                    weights = pool_w[:, :, :].rearrange("p (h r) k -> p k h r", h=tpr)
                    dve.tensor_tensor(weights[:, 0, :, :],
                                      ps_pool[:, 8:8 + TILES].rearrange("p (h r) -> p h r", h=tpr), mask, ALU.mult)
                    dve.tensor_copy(weights[:, 1, :, :], mask).then_inc(pool_w_ready, 1)
                n = t - 3
                if there(n, steps):
                    wait(dve, scores_done, n + 1)
                    wait(dve, rows_done, n)
                    dve.scalar_tensor_tensor(out=masked[:, :].rearrange("p (h r) -> p h r", h=tpr),
                                             in0=ps_soft[:, 0:TILES].rearrange("p (h r) -> p h r", h=tpr),
                                             scalar=0.5, in1=addend[:, 0:tpr, bass.ds(n * rows, rows)],
                                             op0=ALU.mult, op1=ALU.add).then_inc(masked_ready, 1)
                n, k = t, j % 2
                if there(n, steps):
                    wait(dve, hist_flipped, n + 1)
                    wait(dve, z1_done, M1 * (n - 1))
                    dve.tensor_copy(hist_t[:, k, :], ps_hist[:, :]).then_inc(hist_taken, 1)
                n = t - 3
                if there(n, steps):
                    wait(dve, rows_done, n + 1)
                    wait(dve, exps_ready, n)
                    dve.tensor_reduce(neg_max[0:rows, :], ps_soft[0:rows, 256:256 + width], AX.X, ALU.max,
                                      negate=True).then_inc(max_ready, 1)
                n = t - 4
                if there(n, steps):
                    wait(dve, pooled, n + 1)
                    dve.tensor_copy(pooled_t[:, :, bass.ds(n * rows, rows)],
                                    ps_pool[:, 0:2 * rows].rearrange("p (r k) -> p k r", k=2)).then_inc(pooled_taken, 1)
                n = t - 3
                if there(n, steps):
                    wait(dve, exps_ready, n + 1)
                    dve.reciprocal(inv_sum[0:rows, :], exp_sum[0:rows, :]).then_inc(inv_ready, 1)
                    wait(dve, inv_ready, n + 1)
                    wait(dve, probs_flipped, n)
                    dve.tensor_scalar(probs[0:rows, 0:width], exps[0:rows, 0:width], inv_sum[0:rows, :], None,
                                      ALU.mult).then_inc(probs_ready, 1)

            walk(dve, steps, tick)

        @block.vector
        def _(dve):
            chained = 0

            def chain(ins, more=False):
                nonlocal chained
                chained += 1
                ins.then_inc(vec, 1)
                if not more:
                    dve.wait_ge(vec, chained)

            def flip(x):
                return x.rearrange("s (p c) -> s c p", c=C)

            def unflip(x):
                return x.rearrange("s (c p) -> s c p", c=C)

            chain(dve.memset(user_t[E:P, :], 0.0), True)
            chain(dve.memset(bn0[E:P, :, 0:1], 0.0), True)
            dve.wait_ge(loaded_own, 48)
            for k, size in enumerate((NU, NM, NC)):
                chain(dve.tensor_scalar(own_wrap[:, k, :], own_raw[:, k, :], 0, size, ALU.is_lt, ALU.mult), k < 2)
            chain(dve.tensor_tensor(own_sum[:, :, :], own_wrap[:, :, :], own_raw[:, :, :], ALU.add))
            for k, size in enumerate((NU, NM, NC)):
                dve.tensor_scalar(own_idx[:, k, :], own_sum[:, k, :], 0, size - 1,
                                  ALU.max, ALU.min).then_inc(own_idx_ready, 1)
            dve.wait_ge(loaded_tok, 48)
            dve.wait_ge(consts_ready, 3)
            dve.tensor_copy(tok[:, 2, :, 0:T], tok_raw[:, 2, :, :]).then_inc(tok_ready, 1)
            for k, size in enumerate((NM, NC)):
                chain(dve.tensor_scalar(tok_wrap[:, k, :, :], tok_raw[:, k, :, :], 0, size, ALU.is_lt, ALU.mult))
                chain(dve.tensor_tensor(tok_sum[:, k, :, :], tok_wrap[:, k, :, :], tok_raw[:, k, :, :], ALU.add))
                dve.tensor_scalar(tok[:, k, :, 0:T], tok_sum[:, k, :, :], 0, size - 1,
                                  ALU.max, ALU.min).then_inc(tok_ready, 1)
            dve.wait_ge(loaded_lau, 96)
            dve.tensor_scalar(w3_wide[:, :], ones[:, :], w3_sb[:, :], None, ALU.mult).then_inc(params_ready, 1)
            dve.tensor_tensor(w_cur[:, :], w1_raw[:, 0, :], w1_raw[:, 2, :], ALU.add).then_inc(params_ready, 1)
            chain(dve.tensor_tensor(w_base[:, :], w1_raw[:, 1, :], w1_raw[:, 2, :], ALU.subtract), True)
            chain(dve.tensor_scalar(b1_half[:, :], b1_col[:, :], 0.5, None, ALU.mult), True)
            chain(dve.tensor_scalar(b2_half[:, :], b2_col[:, :], 0.5, None, ALU.mult))
            for h in range(HALVES):
                dve.wait_ge(flipped, h + 1)
                dve.tensor_copy(flip(slot_mask[:, h, :]), unflip(ps_z1[0][h][:, :])).then_inc(taken, 1)
            for k in range(2):
                for h in range(HALVES):
                    dve.wait_ge(flipped, 2 * k + h + 3)
                    dve.tensor_copy(flip(slot_idx[:, k, h, :]), unflip(ps_z1[0][h][:, :])).then_inc(taken, 1)
            dve.wait_ge(flipped, 7)
            chain(dve.scalar_tensor_tensor(out=z2_bias[:, :], in0=ps_z2[:, 0:1], scalar=0.25, in1=b2_half[:, :],
                                           op0=ALU.mult, op1=ALU.add), True)
            chain(dve.scalar_tensor_tensor(out=score_bias[:, :], in0=ps_z2[:, 1:2], scalar=0.5, in1=b3_all[:, :],
                                           op0=ALU.mult, op1=ALU.add))
            dve.wait_ge(flipped, 8)
            dve.tensor_copy(flip(cur_t[:, :]), unflip(ps_hist[:, :])).then_inc(taken, 1)
            chain(dve.tensor_scalar(addend_neg[:, :, :], slot_mask[:, :, :], -1.0, -NEG, ALU.add, ALU.mult))
            chain(dve.scalar_tensor_tensor(out=addend[:, :, :], in0=slot_mask[:, :, :], scalar=score_bias[:, :],
                                           in1=addend_neg[:, :, :], op0=ALU.mult, op1=ALU.add), True)
            for m in range(M1):
                dve.wait_ge(flipped, 9 + m)
                dve.tensor_scalar(z1_bias[:, m, :], ps_z1[1][m][:, :], 0.5, b1_half[:, m:m + 1],
                                  ALU.mult, ALU.add).then_inc(setup_done, 1)
            dve.wait_ge(setup_done, M1)
            dve.wait_ge(vec, chained)

            vector_loop(dve, HALVES)

            dve.wait_ge(mlp_done, 1)
            chain(dve.reciprocal(inv_count[:, :], ps_hist[:, :]))
            dve.wait_ge(pooled_taken, B // (TILES // HALVES))
            chain(dve.tensor_tensor(mean_t[:, :], pooled_t[:, 1, :], inv_count[:, :], ALU.mult), True)
            dve.wait_ge(mlp_done, 2)
            chain(dve.tensor_copy(flip(user_t[0:E, :]), unflip(ps_z2[0:E, :])))
            dve.wait_ge(loaded_mlp, LOADED_MLP)

            def batch_norm(first, sources, outs, affine, turn):
                count = len(sources)
                cols = slice(first, first + count)
                for k, x in enumerate(sources):
                    chain(dve.bn_stats(bn_raw[:, first + k, :], x), k < count - 1)
                for k in range(count):
                    chain(dve.bn_aggr(bn_mv[:, first + k, :], bn_raw[:, first + k, :]), k < count - 1)
                dve.tensor_scalar(bn_eps[:, cols], bn_mv[:, cols, 1], EPS, None, ALU.add).then_inc(eps_ready, 1)
                dve.wait_ge(std_ready, turn + 1)
                chain(dve.reciprocal(bn_inv[:, cols], bn_std[:, cols]))
                chain(dve.tensor_tensor(bn_scale[:, cols], bn_inv[:, cols], affine[:, 0, :], ALU.mult))
                chain(dve.tensor_tensor(bn_ms[:, cols], bn_mv[:, cols, 0], bn_scale[:, cols], ALU.mult))
                chain(dve.tensor_tensor(bn_shift[:, cols], affine[:, 1, :], bn_ms[:, cols], ALU.subtract))
                for k, x in enumerate(sources):
                    chain(dve.tensor_scalar(outs[k], x, bn_scale[:, first + k:first + k + 1],
                                            bn_shift[:, first + k:first + k + 1], ALU.mult, ALU.add), k < count - 1)

            def leaky(out_, in_, count):
                for k in range(count):
                    last = dve.scalar_tensor_tensor(out=out_[:, k, :], in0=in_[:, k, :], scalar=0.1,
                                                    in1=in_[:, k, :], op0=ALU.mult, op1=ALU.max)
                last.then_inc(x_ready, 1)

            batch_norm(0, [user_t[:, :], cur_t[:, :], pooled_t[:, 0, :], mean_t[:, :]],
                       [x0[:, k, :] for k in range(4)], bn0, 0)
            dve.sem_inc(x_ready, 1)
            dve.wait_ge(mlp_taken, 4)
            batch_norm(4, [y1[:, k, :] for k in range(4)], [y1n[:, k, :] for k in range(4)], bn1, 1)
            leaky(x1, y1n, 4)
            dve.wait_ge(mlp_taken, 6)
            batch_norm(8, [y2[:, k, :] for k in range(2)], [y2n[:, k, :] for k in range(2)], bn2, 2)
            leaky(x2, y2n, 2)
            dve.wait_ge(mlp_done, 9)
            for c in range(C):
                last = dve.tensor_tensor(result[:, c, :], ps_pool[:, c * NOUT:(c + 1) * NOUT], mb3[:, :], ALU.add)
            last.then_inc(x_ready, 1)


_INS = ["r_uid", "r_mid", "r_cat", "r_historical_mid", "r_historical_cat", "r_mask"] + ["L0_rec_" + n for n in (
    "user_table", "mat_table", "cat_table", "lau_w1", "lau_b1", "lau_w2", "lau_b2", "lau_w3", "lau_b3", "bn0_g",
    "bn0_b", "mlp_w1", "mlp_b1", "bn1_g", "bn1_b", "mlp_w2", "mlp_b2", "bn2_g", "bn2_b", "mlp_w3", "mlp_b3")]


def kernel(**inputs):
    import numpy as np
    import concourse.bacc as bacc
    from concourse.bass_utils import run_bass_kernel_spmd

    nc = bacc.Bacc("TRN2", target_bir_lowering=False, num_devices=1)
    arrays, args = {}, []
    for name in _INS:
        a = np.ascontiguousarray(inputs[name])
        arrays[f"in_{name}"] = a
        args.append(nc.dram_tensor(f"in_{name}", a.shape, mybir.dt.from_np(a.dtype), kind="ExternalInput").ap())
    out = nc.dram_tensor("out", (B, NOUT), F32, kind="ExternalOutput").ap()
    rec_kernel(nc, *args, out)
    r = run_bass_kernel_spmd(nc, [arrays], core_ids=[0])
    return r.results[0]["out"]
```

```python
from contextlib import ExitStack

import concourse.bass as bass
from concourse import mybir

F32 = mybir.dt.float32
I32 = mybir.dt.int32
ALU = mybir.AluOpType
ACT = mybir.ActivationFunctionType
AX = mybir.AxisListType

P = 128
B, T, E = 512, 200, 64
D = 2 * E
C = B // P
H1, H2 = 256, 128
M1 = H1 // P
HALVES = 2
SLOTS = HALVES * P
TILES = 4
COLS = TILES * P
BODY = 8
LAG = 4
F1, F2, NOUT = 512, 256, 2
GROUPS = (slice(0, 1), slice(1, C))
EPS = 1e-5
NEG = -2.0 ** 31
CHUNKS = [(0, E), (E, D), (E + D, D), (E + 2 * D, D)]


def rec_kernel(nc, r_uid, r_mid, r_cat, r_historical_mid, r_historical_cat, r_mask, user_table,
               mat_table, cat_table, lau_w1, lau_b1, lau_w2, lau_b2, lau_w3, lau_b3, bn0_g, bn0_b,
               mlp_w1, mlp_b1, bn1_g, bn1_b, mlp_w2, mlp_b2, bn2_g, bn2_b, mlp_w3, mlp_b3, out):
    NU, NM, NC = user_table.shape[0], mat_table.shape[0], cat_table.shape[0]
    CAT_BITS = (NC - 1).bit_length()
    assert CAT_BITS + (NM - 1).bit_length() < 32
    ctx = ExitStack()
    with ctx:
        ctx.enter_context(nc.allow_non_contiguous_dma(reason="small vectors of parameters"))

        def sb(name, shape, dt=F32):
            return ctx.enter_context(nc.sbuf_tensor(name, shape, dt))

        def bank(name):
            return ctx.enter_context(nc.psum_tensor(name, [P, 512], F32))

        def sem(name):
            return ctx.enter_context(nc.semaphore(name))

        ident = sb("ident", [P, P])
        ones = sb("ones", [P, P])
        ones_t = sb("ones_t", [P, T])
        w1_raw = sb("w1_raw", [P, 4, H1])
        w_base = sb("w_base", [P, H1])
        w_cur = sb("w_cur", [P, H1])
        w_prod = w1_raw[:, 3, :]
        b1_col = sb("b1_col", [P, M1])
        b1_half = sb("b1_half", [P, M1])
        w2_sb = sb("w2_sb", [P, M1, H2])
        b2_col = sb("b2_col", [P, 1])
        b2_half = sb("b2_half", [P, 1])
        z2_bias = sb("z2_bias", [P, 1])
        w3_sb = sb("w3_sb", [P, 1])
        w3_wide = sb("w3_wide", [P, P])
        b3_all = sb("b3_all", [P, 1])
        score_bias = sb("score_bias", [P, 1])
        bn0 = sb("bn0", [P, 2, 4])
        bn1 = sb("bn1", [P, 2, 4])
        bn2 = sb("bn2", [P, 2, 2])
        mw1 = sb("mw1", [P, 4, F1])
        mb1 = sb("mb1", [P, 4])
        mw2 = sb("mw2", [P, 4, F2])
        mb2 = sb("mb2", [P, 2])
        mw3 = sb("mw3", [P, 2, NOUT])
        mb3 = sb("mb3", [P, NOUT])

        own_raw = sb("own_raw", [P, 3, C], I32)
        own_wrap = sb("own_wrap", [P, 3, C])
        own_sum = sb("own_sum", [P, 3, C])
        own_idx = sb("own_idx", [P, 3, C], I32)
        tok_raw = sb("tok_raw", [P, 3, C, T], I32)
        tok_wrap = sb("tok_wrap", [P, 2, C, T])
        tok_clip = sb("tok_clip", [P, 2, C, T])
        tok_int = sb("tok_int", [P, 2, C, T], I32)
        mask_f = sb("mask_f", [P, C, T])
        place = sb("place", [P, C, T])
        gap = sb("gap", [P, C, T])
        shift = sb("shift", [P, 2, C, T], I32)
        moving = sb("moving", [P, C, T], I32)
        key = sb("key", [P, 2, C, T], I32)
        part = tok_int
        tok = sb("tok", [P, 3, C, SLOTS])
        ramp = sb("ramp", [P, SLOTS])
        row_most = sb("row_most", [P, 1])
        most = sb("most", [1, 1], I32)
        slot_idx = sb("slot_idx", [P, 2, HALVES, B], I32)
        slot_mask = sb("slot_mask", [P, HALVES, B])
        addend = sb("addend", [P, HALVES, B])
        addend_neg = sb("addend_neg", [P, HALVES, B])

        own_tok = sb("own_tok", [P, C, D])
        user_tok = sb("user_tok", [P, C, E])
        cur_t = sb("cur_t", [P, B])
        user_t = sb("user_t", [P, B])
        z1_bias = sb("z1_bias", [P, M1, B])

        idx_ring = sb("idx_ring", [P, BODY, 2, TILES], I32)
        hist = sb("hist", [P, BODY, TILES, D])
        hist_t = sb("hist_t", [P, 2, COLS])
        w_row = sb("w_row", [P, 2, TILES, H1])
        t1 = sb("t1", [P, 2, M1, COLS])
        t2 = sb("t2", [P, 2, COLS])
        masked = sb("masked", [P, TILES])
        neg_max = sb("neg_max", [TILES, 1])
        exps = sb("exps", [TILES, SLOTS])
        exp_sum = sb("exp_sum", [TILES, 1])
        inv_sum = sb("inv_sum", [TILES, 1])
        probs = sb("probs", [TILES, SLOTS])
        pool_w = sb("pool_w", [P, TILES, 2])
        pooled_t = sb("pooled_t", [P, 2, B])

        inv_count = sb("inv_count", [P, B])
        mean_t = sb("mean_t", [P, B])
        x0 = sb("x0", [P, 4, B])
        spent = hist[:, :, :, :].rearrange("p s u d -> p (s u d)")
        y1 = spent[:, 0:4 * B].rearrange("p (m b) -> p m b", m=4)
        y1n = spent[:, 4 * B:8 * B].rearrange("p (m b) -> p m b", m=4)
        x1 = t1[:, :, :, :].rearrange("p k m b -> p (k m) b")
        spent_w = w_row[:, :, :, :].rearrange("p k r n -> p (k r n)")
        y2 = spent_w[:, 0:2 * B].rearrange("p (m b) -> p m b", m=2)
        y2n = spent_w[:, 2 * B:4 * B].rearrange("p (m b) -> p m b", m=2)
        x2 = t2
        bn_raw = sb("bn_raw", [P, 10, 6])
        bn_mv = sb("bn_mv", [P, 10, 2])
        bn_eps = sb("bn_eps", [P, 10])
        bn_std = sb("bn_std", [P, 10])
        bn_inv = sb("bn_inv", [P, 10])
        bn_scale = sb("bn_scale", [P, 10])
        bn_ms = sb("bn_ms", [P, 10])
        bn_shift = sb("bn_shift", [P, 10])
        result = sb("result", [P, C, NOUT])

        ps_hist = bank("ps_hist")
        ps_z1 = [[bank(f"ps_z1_{k}_{m}") for m in range(M1)] for k in range(2)]
        ps_z2 = bank("ps_z2")
        ps_soft = bank("ps_soft")
        ps_pool = bank("ps_pool")

        loaded_own = sem("loaded_own")
        loaded_tok = sem("loaded_tok")
        loaded_lau = sem("loaded_lau")
        loaded_mlp = sem("loaded_mlp")
        consts_ready = sem("consts_ready")
        own_idx_ready = sem("own_idx_ready")
        own_gathered = sem("own_gathered")
        user_gathered = sem("user_gathered")
        vec = sem("vec")
        tok_ready = sem("tok_ready")
        flipped = sem("flipped")
        taken = sem("taken")
        setup_done = sem("setup_done")
        params_ready = sem("params_ready")
        most_flipped = sem("most_flipped")
        most_ready = sem("most_ready")
        rest_ready = sem("rest_ready")
        rest_taken = sem("rest_taken")
        counted = sem("counted")

        idx_copied = sem("idx_copied")
        gathered = [sem(f"gathered{k}") for k in range(BODY)]
        hist_flipped = sem("hist_flipped")
        hist_taken = sem("hist_taken")
        w_row_ready = sem("w_row_ready")
        z1_done = sem("z1_done")
        t1_ready = sem("t1_ready")
        z2_done = sem("z2_done")
        t2_ready = sem("t2_ready")
        scores_done = sem("scores_done")
        masked_ready = sem("masked_ready")
        rows_done = sem("rows_done")
        max_ready = sem("max_ready")
        exps_ready = sem("exps_ready")
        inv_ready = sem("inv_ready")
        probs_ready = sem("probs_ready")
        probs_flipped = sem("probs_flipped")
        pool_w_ready = sem("pool_w_ready")
        pooled = sem("pooled")
        pooled_taken = sem("pooled_taken")

        eps_ready = sem("eps_ready")
        std_ready = sem("std_ready")
        x_ready = sem("x_ready")
        mlp_done = sem("mlp_done")
        mlp_taken = sem("mlp_taken")
        stored = sem("stored")

        block = ctx.enter_context(nc.Block())

        def walk(eng, steps, tick, lag=LAG):
            for t in range(BODY):
                tick(t, t)
            with eng.Fori(1, steps // BODY) as i:
                for j in range(BODY):
                    tick(i * BODY + j, j)
            for t in range(steps, steps + lag):
                tick(t, t % BODY)

        def wait(eng, semaphore, count):
            if not isinstance(count, int) or count > 0:
                eng.wait_ge(semaphore, count)

        def there(n, steps):
            return not isinstance(n, int) or 0 <= n < steps

        @block.sync
        def _(sp):
            for k, src in enumerate((r_uid, r_mid, r_cat)):
                sp.dma_start(own_raw[:, k, :], src.rearrange("(p c) -> p c", c=C)).then_inc(loaded_own, 16)
            for k, src in enumerate((r_mask, r_historical_mid, r_historical_cat)):
                sp.dma_start(tok_raw[:, (2, 0, 1)[k], :, :],
                             src.rearrange("(p c) t -> p c t", c=C)).then_inc(loaded_tok, 16)
            sp.dma_start(w1_raw[:, :, :], lau_w1.rearrange("(k p) n -> p k n", p=P)).then_inc(loaded_lau, 16)
            sp.dma_start(b1_col[:, :], lau_b1.rearrange("(m p) -> p m", p=P)).then_inc(loaded_lau, 16)
            sp.dma_start(w2_sb[:, :, :], lau_w2.rearrange("(k p) n -> p k n", p=P)).then_inc(loaded_lau, 16)
            sp.dma_start(b2_col[:, :], lau_b2.rearrange("(p a) -> p a", a=1)).then_inc(loaded_lau, 16)
            sp.dma_start(w3_sb[:, :], lau_w3).then_inc(loaded_lau, 16)
            sp.dma_start(b3_all[:, :], lau_b3.rearrange("(a n) -> a n", a=1).broadcast_to([P, 1])).then_inc(loaded_lau, 16)
            for k, src in enumerate((bn0_g, bn0_b)):
                sp.dma_start(bn0[0:E, k, 0:1], src[0:E].rearrange("(p a) -> p a", a=1)).then_inc(loaded_mlp, 16)
                sp.dma_start(bn0[:, k, 1:4], src[E:].rearrange("(c p) -> p c", p=P)).then_inc(loaded_mlp, 16)
            for k, (g1, g2) in enumerate(((bn1_g, bn2_g), (bn1_b, bn2_b))):
                sp.dma_start(bn1[:, k, :], g1.rearrange("(c p) -> p c", p=P)).then_inc(loaded_mlp, 16)
                sp.dma_start(bn2[:, k, :], g2.rearrange("(c p) -> p c", p=P)).then_inc(loaded_mlp, 16)
            sp.dma_start(mw1[0:E, 0, :], mlp_w1[0:E, :]).then_inc(loaded_mlp, 16)
            sp.dma_start(mw1[:, 1:4, :], mlp_w1[E:, :].rearrange("(c p) n -> p c n", p=P)).then_inc(loaded_mlp, 16)
            sp.dma_start(mb1[:, :], mlp_b1.rearrange("(m p) -> p m", p=P)).then_inc(loaded_mlp, 16)
            sp.dma_start(mw2[:, :, :], mlp_w2.rearrange("(k p) n -> p k n", p=P)).then_inc(loaded_mlp, 16)
            sp.dma_start(mb2[:, :], mlp_b2.rearrange("(m p) -> p m", p=P)).then_inc(loaded_mlp, 16)
            sp.dma_start(mw3[:, :, :], mlp_w3.rearrange("(k p) n -> p k n", p=P)).then_inc(loaded_mlp, 16)
            sp.dma_start(mb3[:, :], mlp_b3.rearrange("(a n) -> a n", a=1).broadcast_to([P, NOUT])).then_inc(loaded_mlp, 16)
            sp.wait_ge(x_ready, 4)
            sp.dma_start(out.rearrange("(p c) n -> p c n", c=C), result[:, :, :]).then_inc(stored, 16)
            sp.wait_ge(stored, 16)
        LOADED_MLP = 16 * 15
        ROW_MOST = 12

        def gather(pool, dst, table, idx, done):
            pool.indirect_dma_start(dst, None, table[:, :],
                                    bass.IndirectOffsetOnAxis(idx, axis=0)).then_inc(done, 16)

        def gather_loop(pool, tpr):
            rows = TILES // tpr
            steps = B // rows

            def copy_idx(n, slot):
                view = idx_ring[:, slot, :, :].rearrange("p k (h r) -> p k h r", h=tpr)
                pool.tensor_copy(view, slot_idx[:, :, 0:tpr, bass.ds(n * rows, rows)]).then_inc(idx_copied, 1)

            def tick(n, slot):
                if not there(n, steps):
                    return
                wait(pool, pooled, n - BODY + 1)
                wait(pool, idx_copied, n + 1)
                if not isinstance(n, int) or n + 1 < steps:
                    after = (slot + 1) % BODY
                    if isinstance(n, int):
                        wait(pool, gathered[after], 128 * ((n + 1) // BODY))
                    else:
                        wait(pool, gathered[after], (n - slot) * 16 + 128 * ((slot + 1) // BODY))
                    copy_idx(n + 1, after)
                for u in range(TILES):
                    r, h = divmod(u, tpr)
                    at = h * rows + r
                    gather(pool, hist[:, slot, u, 0:E], mat_table, idx_ring[:, slot, 0, at:at + 1], gathered[slot])
                    gather(pool, hist[:, slot, u, E:D], cat_table, idx_ring[:, slot, 1, at:at + 1], gathered[slot])

            if tpr == 1:
                pool.wait_ge(taken, 2)
            else:
                pool.wait_ge(rest_taken, 3)
            copy_idx(0, 0)
            for t in range(BODY):
                tick(t, t)
            pool.wait_ge(taken, 5)
            with pool.Fori(1, steps // BODY - 1) as i:
                for j in range(BODY):
                    tick(i * BODY + j, j)
            for t in range(steps - BODY, steps):
                tick(t, t % BODY)

        @block.gpsimd
        def _(pool):
            pool.memset(ident[:, :], 0.0).then_inc(consts_ready, 1)
            pool.memset(ones[:, :], 1.0).then_inc(consts_ready, 1)
            pool.memset(ones_t[:, :], 1.0)
            pool.memset(tok[:, :, :, T:SLOTS], 0.0).then_inc(consts_ready, 1)
            pool.iota(ramp[:, :], [[1, SLOTS]], base=0, channel_multiplier=0,
                      allow_small_or_imprecise_dtypes=True).then_inc(consts_ready, 1)
            pool.wait_ge(consts_ready, 4)
            pool.affine_select(out=ident[:, :], in_=ident[:, :], compare_op=ALU.not_equal, fill=1.0,
                               base=0, pattern=[[-1, P]], channel_multiplier=1).then_inc(consts_ready, 1)
            pool.wait_ge(own_idx_ready, 3)
            for c in range(C):
                gather(pool, own_tok[:, c, 0:E], mat_table, own_idx[:, 1, c:c + 1], own_gathered)
                gather(pool, own_tok[:, c, E:D], cat_table, own_idx[:, 2, c:c + 1], own_gathered)
            pool.wait_ge(most_ready, 1)
            with pool.If(pool.value_load(most[0:1, 0:1], min_val=0, max_val=T) > P):
                gather_loop(pool, HALVES)
            with pool.Else():
                gather_loop(pool, 1)
            for c in range(C):
                gather(pool, user_tok[:, c, :], user_table, own_idx[:, 0, c:c + 1], user_gathered)

        def tensor_loop(pe, tpr):
            rows = TILES // tpr
            width = tpr * P
            steps = B // rows
            score_cols = ps_soft[:, 0:TILES]
            prob_cols = ps_pool[:, 8:8 + TILES]
            row_major = ps_soft[0:rows, 256:256 + width]

            def tick(t, j):
                n, k = t - 1, (j - 1) % 2
                if there(n, steps):
                    wait(pe, hist_taken, n + 1)
                    wait(pe, w_row_ready, n + 1)
                    wait(pe, t1_ready, M1 * (n - 1))
                    for m in range(M1):
                        for r in range(rows):
                            last = pe.matmul(ps_z1[k][m][:, r * width:(r + 1) * width],
                                             w_row[:, k, r, m * P:(m + 1) * P],
                                             hist_t[:, k, r * width:(r + 1) * width], start=True, stop=True)
                        last.then_inc(z1_done, 1)
                n = t - 4
                if there(n, steps):
                    wait(pe, probs_ready, n + 1)
                    wait(pe, pooled_taken, n)
                    pe.nop(nofuse=True)
                    for h in range(tpr):
                        last = pe.transpose(prob_cols[:, h * rows:(h + 1) * rows],
                                            probs[0:rows, h * P:(h + 1) * P], ident[0:rows, 0:rows])
                    last.then_inc(probs_flipped, 1)
                n, k = t - 3, (j - 3) % 2
                if there(n, steps):
                    wait(pe, t2_ready, n + 1)
                    wait(pe, exps_ready, n)
                    for u in range(TILES):
                        r, h = divmod(u, tpr)
                        at = h * rows + r
                        last = pe.matmul(score_cols[:, at:at + 1], t2[:, k, u * P:(u + 1) * P], w3_sb[:, :],
                                         start=True, stop=True)
                    last.then_inc(scores_done, 1)
                n = t
                if there(n, steps):
                    wait(pe, gathered[j], 128 * (n // BODY + 1) if isinstance(n, int) else (n - j) * 16 + 128)
                    wait(pe, hist_taken, n)
                    for u in range(TILES):
                        last = pe.transpose(ps_hist[:, u * P:(u + 1) * P], hist[:, j, u, :], ident[:, :])
                    last.then_inc(hist_flipped, 1)
                n, k = t - 2, (j - 2) % 2
                if there(n, steps):
                    wait(pe, t1_ready, M1 * (n + 1))
                    wait(pe, t2_ready, n)
                    for m in range(M1):
                        last = pe.matmul(ps_z2[:, :], w2_sb[:, m, :], t1[:, k, m, :],
                                         start=(m == 0), stop=(m == M1 - 1))
                    last.then_inc(z2_done, 1)
                n = t - 3
                if there(n, steps):
                    wait(pe, masked_ready, n + 1)
                    for h in range(tpr):
                        last = pe.transpose(row_major[:, h * P:(h + 1) * P],
                                            masked[:, h * rows:(h + 1) * rows], ident[:, :])
                    last.then_inc(rows_done, 1)
                n, slot = t - 4, (j - 4) % BODY
                if there(n, steps):
                    wait(pe, pool_w_ready, n + 1)
                    for r in range(rows):
                        for h in range(tpr):
                            last = pe.matmul(ps_pool[:, 2 * r:2 * r + 2], hist[:, slot, r * tpr + h, :],
                                             pool_w[:, h * rows + r, :], start=(h == 0), stop=(h == tpr - 1))
                    last.then_inc(pooled, 1)

            walk(pe, steps, tick)
            pe.wait_ge(hist_taken, steps)
            for h in range(tpr):
                last = pe.matmul(ps_hist[:, :], ones[:, :], slot_mask[:, h, :], start=(h == 0), stop=(h == tpr - 1))
            last.then_inc(counted, 1)

        @block.tensor
        def _(pe):
            pe.wait_ge(consts_ready, 5)
            pe.wait_ge(vec, ROW_MOST)
            pe.transpose(ps_soft[0:1, 0:P], row_most[:, :], ident[:, :]).then_inc(most_flipped, 1)
            pe.wait_ge(tok_ready, 1)
            for k in range(3):
                last = pe.transpose(ps_z1[0][0][:, k * P:(k + 1) * P], tok[:, k, 0, 0:P], ident[:, :])
            last.then_inc(flipped, 1)
            pe.wait_ge(tok_ready, 2)
            for k in range(3):
                for c in range(1, C):
                    last = pe.transpose((ps_z1[0][1], ps_z1[1][0], ps_z1[1][1])[k][:, (c - 1) * P:c * P],
                                        tok[:, k, c, 0:P], ident[:, :])
                last.then_inc(flipped, 1)
            pe.wait_ge(loaded_lau, 96)
            pe.wait_ge(params_ready, 1)
            for m in range(M1):
                pe.matmul(ps_z2[:, 0:1], w2_sb[:, m, :], ones[:, 0:1], start=(m == 0), stop=(m == M1 - 1))
            pe.matmul(ps_z2[:, 1:2], w3_wide[:, :], ones[:, 0:1], start=True, stop=True).then_inc(flipped, 1)
            pe.wait_ge(own_gathered, 16 * 2 * C)
            for c in range(C):
                last = pe.transpose(ps_hist[:, c * P:(c + 1) * P], own_tok[:, c, :], ident[:, :])
            last.then_inc(flipped, 1)
            pe.wait_ge(taken, 6)
            pe.wait_ge(params_ready, 2)
            for m in range(M1):
                last = pe.matmul(ps_z1[1][m][:, :], w_cur[:, m * P:(m + 1) * P], cur_t[:, :], start=True, stop=True)
                last.then_inc(flipped, 1)
            pe.wait_ge(setup_done, M1)
            pe.wait_ge(most_ready, 1)
            with pe.If(pe.value_load(most[0:1, 0:1], min_val=0, max_val=T) > P):
                for k in range(3):
                    for c in range(C):
                        last = pe.transpose((ps_z1[0][0], ps_z1[0][1], ps_z1[1][0])[k][:, c * P:(c + 1) * P],
                                            tok[:, k, c, P:SLOTS], ident[:, :])
                    last.then_inc(rest_ready, 1)
                pe.wait_ge(rest_taken, 3)
                tensor_loop(pe, HALVES)
            with pe.Else():
                tensor_loop(pe, 1)
            pe.wait_ge(user_gathered, 16 * C)
            for c in range(C):
                last = pe.transpose(ps_z2[0:E, c * P:(c + 1) * P], user_tok[:, c, :], ident[:, :])
            last.then_inc(mlp_done, 1)
            pe.wait_ge(x_ready, 1)
            pe.wait_ge(loaded_mlp, LOADED_MLP)
            for m in range(4):
                for k, (_, size) in enumerate(CHUNKS):
                    last = pe.matmul(ps_z1[m // 2][m % 2][:, :], mw1[0:size, k, m * P:(m + 1) * P],
                                     x0[0:size, k, :], start=(k == 0), stop=(k == 3))
                last.then_inc(mlp_done, 1)
            pe.wait_ge(x_ready, 2)
            for m in range(2):
                for k in range(4):
                    last = pe.matmul((ps_z2, ps_hist)[m][:, :], mw2[:, k, m * P:(m + 1) * P], x1[:, k, :],
                                     start=(k == 0), stop=(k == 3))
                last.then_inc(mlp_done, 1)
            pe.wait_ge(x_ready, 3)
            for c in range(C):
                for k in range(2):
                    last = pe.matmul(ps_pool[:, c * NOUT:(c + 1) * NOUT], x2[:, k, c * P:(c + 1) * P], mw3[:, k, :],
                                     start=(k == 0), stop=(k == 1))
            last.then_inc(mlp_done, 1)

        def scalar_loop(act, tpr):
            rows = TILES // tpr
            width = tpr * P
            steps = B // rows

            def tick(t, j):
                n, k = t - 1, (j - 1) % 2
                if there(n, steps):
                    wait(act, z2_done, n - 1)
                    for m in range(M1):
                        wait(act, z1_done, M1 * n + m + 1)
                        for r in range(rows):
                            last = act.activation(t1[:, k, m, r * width:(r + 1) * width],
                                                  ps_z1[k][m][:, r * width:(r + 1) * width], ACT.Tanh,
                                                  bias=z1_bias[:, m, bass.ds(n * rows + r, 1)], scale=0.5)
                        last.then_inc(t1_ready, 1)
                n, k = t - 2, (j - 2) % 2
                if there(n, steps):
                    wait(act, z2_done, n + 1)
                    wait(act, scores_done, n - 1)
                    act.activation(t2[:, k, :], ps_z2[:, :], ACT.Tanh, bias=z2_bias[:, :],
                                   scale=0.25).then_inc(t2_ready, 1)
                n = t - 3
                if there(n, steps):
                    wait(act, max_ready, n + 1)
                    wait(act, probs_ready, n)
                    act.activation(exps[0:rows, 0:width], ps_soft[0:rows, 256:256 + width], ACT.Exp,
                                   bias=neg_max[0:rows, :], accum_out=exp_sum[0:rows, :]).then_inc(exps_ready, 1)

            walk(act, steps, tick)

        @block.scalar
        def _(act):
            act.wait_ge(setup_done, M1)
            act.wait_ge(most_ready, 1)
            with act.If(act.value_load(most[0:1, 0:1], min_val=0, max_val=T) > P):
                scalar_loop(act, HALVES)
            with act.Else():
                scalar_loop(act, 1)

            def std(first, count, need):
                act.wait_ge(eps_ready, need)
                act.activation(bn_std[:, first:first + count], bn_eps[:, first:first + count],
                               ACT.Sqrt).then_inc(std_ready, 1)

            std(0, 4, 1)
            for m in range(4):
                act.wait_ge(mlp_done, 2 + m)
                act.activation(y1[:, m, :], ps_z1[m // 2][m % 2][:, :], ACT.Identity,
                               bias=mb1[:, m:m + 1]).then_inc(mlp_taken, 1)
            std(4, 4, 2)
            for m in range(2):
                act.wait_ge(mlp_done, 6 + m)
                act.activation(y2[:, m, :], (ps_z2, ps_hist)[m][:, :], ACT.Identity,
                               bias=mb2[:, m:m + 1]).then_inc(mlp_taken, 1)
            std(8, 2, 3)

        def vector_loop(dve, tpr):
            rows = TILES // tpr
            width = tpr * P
            steps = B // rows

            def tick(t, j):
                n, k = t, j % 2
                if there(n, steps):
                    wait(dve, z1_done, M1 * (n - 1))
                    for r in range(rows):
                        last = dve.scalar_tensor_tensor(out=w_row[:, k, r, :], in0=w_prod,
                                                        scalar=cur_t[:, bass.ds(n * rows + r, 1)],
                                                        in1=w_base[:, :], op0=ALU.mult, op1=ALU.add)
                    last.then_inc(w_row_ready, 1)
                n = t - 4
                if there(n, steps):
                    wait(dve, probs_flipped, n + 1)
                    wait(dve, pooled, n)
                    mask = slot_mask[:, 0:tpr, bass.ds(n * rows, rows)]
                    weights = pool_w[:, :, :].rearrange("p (h r) k -> p k h r", h=tpr)
                    dve.tensor_tensor(weights[:, 0, :, :],
                                      ps_pool[:, 8:8 + TILES].rearrange("p (h r) -> p h r", h=tpr), mask, ALU.mult)
                    dve.tensor_copy(weights[:, 1, :, :], mask).then_inc(pool_w_ready, 1)
                n = t - 3
                if there(n, steps):
                    wait(dve, scores_done, n + 1)
                    wait(dve, rows_done, n)
                    dve.scalar_tensor_tensor(out=masked[:, :].rearrange("p (h r) -> p h r", h=tpr),
                                             in0=ps_soft[:, 0:TILES].rearrange("p (h r) -> p h r", h=tpr),
                                             scalar=0.5, in1=addend[:, 0:tpr, bass.ds(n * rows, rows)],
                                             op0=ALU.mult, op1=ALU.add).then_inc(masked_ready, 1)
                n, k = t, j % 2
                if there(n, steps):
                    wait(dve, hist_flipped, n + 1)
                    wait(dve, z1_done, M1 * (n - 1))
                    dve.tensor_copy(hist_t[:, k, :], ps_hist[:, :]).then_inc(hist_taken, 1)
                n = t - 3
                if there(n, steps):
                    wait(dve, rows_done, n + 1)
                    wait(dve, exps_ready, n)
                    dve.tensor_reduce(neg_max[0:rows, :], ps_soft[0:rows, 256:256 + width], AX.X, ALU.max,
                                      negate=True).then_inc(max_ready, 1)
                n = t - 4
                if there(n, steps):
                    wait(dve, pooled, n + 1)
                    dve.tensor_copy(pooled_t[:, :, bass.ds(n * rows, rows)],
                                    ps_pool[:, 0:2 * rows].rearrange("p (r k) -> p k r", k=2)).then_inc(pooled_taken, 1)
                n = t - 3
                if there(n, steps):
                    wait(dve, exps_ready, n + 1)
                    dve.reciprocal(inv_sum[0:rows, :], exp_sum[0:rows, :]).then_inc(inv_ready, 1)
                    wait(dve, inv_ready, n + 1)
                    wait(dve, probs_flipped, n)
                    dve.tensor_scalar(probs[0:rows, 0:width], exps[0:rows, 0:width], inv_sum[0:rows, :], None,
                                      ALU.mult).then_inc(probs_ready, 1)

            walk(dve, steps, tick)
            dve.wait_ge(pooled_taken, steps)

        @block.vector
        def _(dve):
            chained = 0

            def chain(ins, more=False):
                nonlocal chained
                chained += 1
                ins.then_inc(vec, 1)
                if not more:
                    dve.wait_ge(vec, chained)

            chain(dve.memset(user_t[E:P, :], 0.0), True)
            chain(dve.memset(bn0[E:P, :, 0:1], 0.0), True)
            dve.wait_ge(loaded_own, 48)
            for k, size in enumerate((NU, NM, NC)):
                chain(dve.tensor_scalar(own_wrap[:, k, :], own_raw[:, k, :], 0, size, ALU.is_lt, ALU.mult), k < 2)
            chain(dve.tensor_tensor(own_sum[:, :, :], own_wrap[:, :, :], own_raw[:, :, :], ALU.add))
            for k, size in enumerate((NU, NM, NC)):
                dve.tensor_scalar(own_idx[:, k, :], own_sum[:, k, :], 0, size - 1,
                                  ALU.max, ALU.min).then_inc(own_idx_ready, 1)
            dve.wait_ge(loaded_tok, 16 * 3)
            chain(dve.tensor_copy(mask_f[:, :, :], tok_raw[:, 2, :, :]))
            dve.wait_ge(consts_ready, 4)
            for c in range(C):
                chain(dve.tensor_tensor_scan(place[:, c, :], ones_t[:, :], mask_f[:, c, :], 0.0,
                                             ALU.mult, ALU.add), c < C - 1)
            chain(dve.tensor_reduce(row_most[:, :], place[:, :, T - 1], AX.X, ALU.max))
            assert chained == ROW_MOST

            def compact(group):
                at = (slice(None), group)
                cols = group.stop - group.start
                clear = (slice(None), slice(None), group)
                for k, size in enumerate((NM, NC)):
                    chain(dve.tensor_scalar(tok_wrap[:, k, group, :], tok_raw[:, k, group, :], 0, size,
                                            ALU.is_lt, ALU.mult), True)
                    chain(dve.tensor_scalar(tok_clip[:, k, group, :], tok_raw[:, k, group, :], -size, size - 1,
                                            ALU.max, ALU.min), True)
                for c in range(group.start, group.stop):
                    chain(dve.scalar_tensor_tensor(out=gap[:, c, :], in0=ramp[:, 0:T], scalar=1.0,
                                                   in1=place[:, c, :], op0=ALU.add, op1=ALU.subtract),
                          c < group.stop - 1)
                for k in range(2):
                    chain(dve.tensor_tensor(tok_int[:, k, group, :], tok_clip[:, k, group, :],
                                            tok_wrap[:, k, group, :], ALU.add), True)
                chain(dve.tensor_tensor(shift[:, 0, group, :], gap[at], mask_f[at], ALU.mult))
                chain(dve.scalar_tensor_tensor(out=key[:, 0, group, :], in0=tok_int[:, 0, group, :], scalar=CAT_BITS,
                                               in1=tok_int[:, 1, group, :], op0=ALU.logical_shift_left,
                                               op1=ALU.bitwise_or), True)
                for bit in range((T - 1).bit_length()):
                    by, old, new = 1 << bit, bit % 2, 1 - bit % 2
                    chain(dve.tensor_scalar(moving[at], shift[:, old, group, :], by, None, ALU.bitwise_and))
                    chain(dve.scalar_tensor_tensor(out=shift[:, new, group, :], in0=moving[at], scalar=0,
                                                   in1=shift[:, old, group, :], op0=ALU.is_equal, op1=ALU.mult), True)
                    chain(dve.tensor_copy(key[:, new, group, :], key[:, old, group, :]))
                    chain(dve.copy_predicated(shift[:, new, group, 0:T - by], moving[:, group, by:T],
                                              shift[:, old, group, by:T]), True)
                    chain(dve.copy_predicated(key[:, new, group, 0:T - by], moving[:, group, by:T],
                                              key[:, old, group, by:T]))
                end = (T - 1).bit_length() % 2
                chain(dve.tensor_single_scalar(part[:, 0, group, :], key[:, end, group, :], CAT_BITS,
                                               ALU.logical_shift_right), True)
                chain(dve.tensor_single_scalar(part[:, 1, group, :], key[:, end, group, :], (1 << CAT_BITS) - 1,
                                               ALU.bitwise_and), True)
                for c in range(group.start, group.stop):
                    chain(dve.tensor_scalar(tok[:, 2, c, :], ramp[:, :], place[:, c, T - 1:T], None, ALU.is_lt),
                          c < group.stop - 1)
                for k in range(2):
                    last = dve.tensor_copy(tok[:, k, group, 0:T], part[:, k, group, :])
                last.then_inc(tok_ready, 1)

            compact(GROUPS[0])
            dve.wait_ge(most_flipped, 1)
            chain(dve.tensor_reduce(most[:, :], ps_soft[0:1, 0:P], AX.X, ALU.max))
            dve.sem_inc(most_ready, 1)
            dve.wait_ge(flipped, 1)
            dve.tensor_copy(slot_idx[:, :, 0, 0:P],
                            ps_z1[0][0][:, 0:2 * P].rearrange("p (k b) -> p k b", k=2)).then_inc(taken, 1)
            dve.tensor_copy(slot_mask[:, 0, 0:P], ps_z1[0][0][:, 2 * P:3 * P]).then_inc(taken, 1)
            compact(GROUPS[1])
            for k in range(2):
                dve.wait_ge(flipped, 2 + k)
                dve.tensor_copy(slot_idx[:, k, 0, P:B], (ps_z1[0][1], ps_z1[1][0])[k][:, 0:B - P]).then_inc(taken, 1)
            dve.wait_ge(flipped, 4)
            dve.tensor_copy(slot_mask[:, 0, P:B], ps_z1[1][1][:, 0:B - P]).then_inc(taken, 1)
            dve.wait_ge(loaded_lau, 96)
            dve.tensor_scalar(w3_wide[:, :], ones[:, :], w3_sb[:, :], None, ALU.mult).then_inc(params_ready, 1)
            dve.tensor_tensor(w_cur[:, :], w1_raw[:, 0, :], w1_raw[:, 2, :], ALU.add).then_inc(params_ready, 1)
            chain(dve.tensor_tensor(w_base[:, :], w1_raw[:, 1, :], w1_raw[:, 2, :], ALU.subtract), True)
            chain(dve.tensor_scalar(b1_half[:, :], b1_col[:, :], 0.5, None, ALU.mult), True)
            chain(dve.tensor_scalar(b2_half[:, :], b2_col[:, :], 0.5, None, ALU.mult))
            dve.wait_ge(flipped, 5)
            chain(dve.scalar_tensor_tensor(out=z2_bias[:, :], in0=ps_z2[:, 0:1], scalar=0.25, in1=b2_half[:, :],
                                           op0=ALU.mult, op1=ALU.add), True)
            chain(dve.scalar_tensor_tensor(out=score_bias[:, :], in0=ps_z2[:, 1:2], scalar=0.5, in1=b3_all[:, :],
                                           op0=ALU.mult, op1=ALU.add))
            dve.wait_ge(flipped, 6)
            dve.tensor_copy(cur_t[:, :], ps_hist[:, :]).then_inc(taken, 1)
            def add_terms(h):
                chain(dve.tensor_scalar(addend_neg[:, h, :], slot_mask[:, h, :], -1.0, -NEG, ALU.add, ALU.mult))
                chain(dve.scalar_tensor_tensor(out=addend[:, h, :], in0=slot_mask[:, h, :], scalar=score_bias[:, :],
                                               in1=addend_neg[:, h, :], op0=ALU.mult, op1=ALU.add))

            dve.wait_ge(taken, 6)
            add_terms(0)
            for m in range(M1):
                dve.wait_ge(flipped, 7 + m)
                dve.tensor_scalar(z1_bias[:, m, :], ps_z1[1][m][:, :], 0.5, b1_half[:, m:m + 1],
                                  ALU.mult, ALU.add).then_inc(setup_done, 1)
            dve.wait_ge(setup_done, M1)
            dve.wait_ge(vec, chained)

            with dve.If(dve.value_load(most[0:1, 0:1], min_val=0, max_val=T) > P):
                for k in range(3):
                    dve.wait_ge(rest_ready, 1 + k)
                    dve.tensor_copy(slot_idx[:, k, 1, :] if k < 2 else slot_mask[:, 1, :],
                                    (ps_z1[0][0], ps_z1[0][1], ps_z1[1][0])[k][:, :]).then_inc(rest_taken, 1)
                dve.wait_ge(rest_taken, 3)
                start = chained
                add_terms(1)
                vector_loop(dve, HALVES)
            with dve.Else():
                dve.sem_inc(vec, chained - start)
                dve.wait_ge(vec, chained)
                vector_loop(dve, 1)

            dve.wait_ge(counted, 1)
            chain(dve.reciprocal(inv_count[:, :], ps_hist[:, :]))
            chain(dve.tensor_tensor(mean_t[:, :], pooled_t[:, 1, :], inv_count[:, :], ALU.mult), True)
            dve.wait_ge(mlp_done, 1)
            chain(dve.tensor_copy(user_t[0:E, :], ps_z2[0:E, :]))
            dve.wait_ge(loaded_mlp, LOADED_MLP)

            def batch_norm(first, sources, outs, affine, turn):
                count = len(sources)
                cols = slice(first, first + count)
                for k, x in enumerate(sources):
                    chain(dve.bn_stats(bn_raw[:, first + k, :], x), k < count - 1)
                for k in range(count):
                    chain(dve.bn_aggr(bn_mv[:, first + k, :], bn_raw[:, first + k, :]), k < count - 1)
                dve.tensor_scalar(bn_eps[:, cols], bn_mv[:, cols, 1], EPS, None, ALU.add).then_inc(eps_ready, 1)
                dve.wait_ge(std_ready, turn + 1)
                chain(dve.reciprocal(bn_inv[:, cols], bn_std[:, cols]))
                chain(dve.tensor_tensor(bn_scale[:, cols], bn_inv[:, cols], affine[:, 0, :], ALU.mult))
                chain(dve.tensor_tensor(bn_ms[:, cols], bn_mv[:, cols, 0], bn_scale[:, cols], ALU.mult))
                chain(dve.tensor_tensor(bn_shift[:, cols], affine[:, 1, :], bn_ms[:, cols], ALU.subtract))
                for k, x in enumerate(sources):
                    chain(dve.tensor_scalar(outs[k], x, bn_scale[:, first + k:first + k + 1],
                                            bn_shift[:, first + k:first + k + 1], ALU.mult, ALU.add), k < count - 1)

            def leaky(out_, in_, count):
                for k in range(count):
                    last = dve.scalar_tensor_tensor(out=out_[:, k, :], in0=in_[:, k, :], scalar=0.1,
                                                    in1=in_[:, k, :], op0=ALU.mult, op1=ALU.max)
                last.then_inc(x_ready, 1)

            batch_norm(0, [user_t[:, :], cur_t[:, :], pooled_t[:, 0, :], mean_t[:, :]],
                       [x0[:, k, :] for k in range(4)], bn0, 0)
            dve.sem_inc(x_ready, 1)
            dve.wait_ge(mlp_taken, 4)
            batch_norm(4, [y1[:, k, :] for k in range(4)], [y1n[:, k, :] for k in range(4)], bn1, 1)
            leaky(x1, y1n, 4)
            dve.wait_ge(mlp_taken, 6)
            batch_norm(8, [y2[:, k, :] for k in range(2)], [y2n[:, k, :] for k in range(2)], bn2, 2)
            leaky(x2, y2n, 2)
            dve.wait_ge(mlp_done, 8)
            for c in range(C):
                last = dve.tensor_tensor(result[:, c, :], ps_pool[:, c * NOUT:(c + 1) * NOUT], mb3[:, :], ALU.add)
            last.then_inc(x_ready, 1)


_INS = ["r_uid", "r_mid", "r_cat", "r_historical_mid", "r_historical_cat", "r_mask"] + ["L0_rec_" + n for n in (
    "user_table", "mat_table", "cat_table", "lau_w1", "lau_b1", "lau_w2", "lau_b2", "lau_w3", "lau_b3", "bn0_g",
    "bn0_b", "mlp_w1", "mlp_b1", "bn1_g", "bn1_b", "mlp_w2", "mlp_b2", "bn2_g", "bn2_b", "mlp_w3", "mlp_b3")]


def kernel(**inputs):
    import numpy as np
    import concourse.bacc as bacc
    from concourse.bass_utils import run_bass_kernel_spmd

    nc = bacc.Bacc("TRN2", target_bir_lowering=False, num_devices=1)
    arrays, args = {}, []
    for name in _INS:
        a = np.ascontiguousarray(inputs[name])
        arrays[f"in_{name}"] = a
        args.append(nc.dram_tensor(f"in_{name}", a.shape, mybir.dt.from_np(a.dtype), kind="ExternalInput").ap())
    out = nc.dram_tensor("out", (B, NOUT), F32, kind="ExternalOutput").ap()
    rec_kernel(nc, *args, out)
    r = run_bass_kernel_spmd(nc, [arrays], core_ids=[0])
    return r.results[0]["out"]
```

```python
from contextlib import ExitStack

import concourse.bass as bass
from concourse import mybir

F32 = mybir.dt.float32
I32 = mybir.dt.int32
BF16 = mybir.dt.bfloat16
F16 = mybir.dt.float16
ALU = mybir.AluOpType
ACT = mybir.ActivationFunctionType
AX = mybir.AxisListType

P = 128
B, T, E = 512, 200, 64
D = 2 * E
C = B // P
H1, H2 = 256, 128
M1 = H1 // P
HALVES = 2
SLOTS = HALVES * P
TILES = 4
COLS = TILES * P
REP = 32
BIG = 2.0 ** 32
BODY = 8
PEEL = 2 * BODY
LAG = 5
AHEAD = 5
BY_PRODUCT = (2,) * BODY
F1, F2, NOUT = 512, 256, 2
GROUPS = (slice(0, 1), slice(1, C))
EPS = 1e-5
CHUNKS = [(0, E), (E, D), (E + D, D), (E + 2 * D, D)]


def rec_kernel(nc, r_uid, r_mid, r_cat, r_historical_mid, r_historical_cat, r_mask, user_table,
               mat_table, cat_table, lau_w1, lau_b1, lau_w2, lau_b2, lau_w3, lau_b3, bn0_g, bn0_b,
               mlp_w1, mlp_b1, bn1_g, bn1_b, mlp_w2, mlp_b2, bn2_g, bn2_b, mlp_w3, mlp_b3, out):
    NU, NM, NC = user_table.shape[0], mat_table.shape[0], cat_table.shape[0]
    CAT_BITS = (NC - 1).bit_length()
    assert CAT_BITS + (NM - 1).bit_length() < 32
    KC = -(-NC // P)
    KP = NC // KC
    assert KC * KP == NC <= 2048
    MOST = max(BY_PRODUCT)
    FIRST_CHUNKS, LAST_CHUNKS = range(KC * 5 // 8), range(KC * 5 // 8, KC)
    ctx = ExitStack()
    with ctx:
        ctx.enter_context(nc.allow_non_contiguous_dma(reason="small vectors of parameters"))

        def sb(name, shape, dt=F32):
            return ctx.enter_context(nc.sbuf_tensor(name, shape, dt))

        def bank(name):
            return ctx.enter_context(nc.psum_tensor(name, [P, 512], F32))

        def sem(name):
            return ctx.enter_context(nc.semaphore(name))

        ident = sb("ident", [P, P])
        ones = sb("ones", [P, P])
        ones_t = sb("ones_t", [P, T])
        w1_raw = sb("w1_raw", [P, 4, H1])
        w_base = sb("w_base", [P, H1])
        w_cur = sb("w_cur", [P, H1])
        w_prod = w1_raw[:, 3, :]
        b1_col = sb("b1_col", [P, M1])
        b1_half = sb("b1_half", [P, M1])
        w2_sb = sb("w2_sb", [P, M1, H2])
        b2_col = sb("b2_col", [P, 1])
        b2_half = sb("b2_half", [P, 1])
        z2_bias = sb("z2_bias", [P, 1])
        w3_sb = sb("w3_sb", [P, 1])
        w3_col = sb("w3_col", [P, 1])
        w3_half = sb("w3_half", [P, P])
        b3_all = sb("b3_all", [P, 1])
        score_bias = sb("score_bias", [P, 1])
        bn0 = sb("bn0", [P, 2, 4])
        bn1 = sb("bn1", [P, 2, 4])
        bn2 = sb("bn2", [P, 2, 2])
        mw1 = sb("mw1", [P, 4, F1])
        mb1 = sb("mb1", [P, 4])
        mw2 = sb("mw2", [P, 4, F2])
        mb2 = sb("mb2", [P, 2])
        mw3 = sb("mw3", [P, 2, NOUT])
        mb3 = sb("mb3", [P, NOUT])
        cat_f = sb("cat_f", [KP, KC, E])
        cat_rest = sb("cat_rest", [KP, 2, KC, E])
        cat_part = sb("cat_part", [KP, KC, 3, E], BF16)
        cat_id = sb("cat_id", [P, KC])

        own_raw = sb("own_raw", [P, 3, C], I32)
        own_wrap = sb("own_wrap", [P, 3, C])
        own_sum = sb("own_sum", [P, 3, C])
        own_idx = sb("own_idx", [P, 3, C], I32)
        tok_raw = sb("tok_raw", [P, 3, C, T], I32)
        tok_wrap = sb("tok_wrap", [P, 2, C, T])
        tok_clip = sb("tok_clip", [P, 2, C, T])
        tok_int = sb("tok_int", [P, 2, C, T], I32)
        mask_f = sb("mask_f", [P, C, T])
        place = sb("place", [P, C, T])
        gap = sb("gap", [P, C, T])
        shift = sb("shift", [P, 2, C, T], I32)
        moving = sb("moving", [P, C, T], I32)
        key = sb("key", [P, 2, C, T], I32)
        part = tok_int
        tok = sb("tok", [P, 3, C, SLOTS])
        cat_small = sb("cat_small", [P, C, SLOTS], F16)
        ramp = sb("ramp", [P, SLOTS])
        count_diag = sb("count_diag", [P, C, P])
        ramp_1 = sb("ramp_1", [P, T])
        row_most = sb("row_most", [P, 1])
        most = sb("most", [1, 1], I32)
        slot_idx = sb("slot_idx", [P, 2, HALVES, B + AHEAD * TILES], I32)
        slot_mask = sb("slot_mask", [P, HALVES, B])
        part_id = sb("part_id", [P, 1], I32)
        upper = sb("upper", [P, 1], I32)
        for_probs = sb("for_probs", [P, 1])
        for_mean = sb("for_mean", [P, 1])
        slot_level = sb("slot_level", [P, SLOTS])
        count_level = sb("count_level", [P, B // 2])
        count_mean = sb("count_mean", [P, B // 2])

        own_tok = sb("own_tok", [P, C, D])
        user_tok = sb("user_tok", [P, C, E])
        cur_t = sb("cur_t", [P, B])
        user_t = sb("user_t", [P, B])
        z1_bias = sb("z1_bias", [P, M1, B])

        idx_ring = sb("idx_ring", [P, BODY, 2, TILES], I32)
        hist = sb("hist", [P, BODY, TILES, D])
        hist_t = sb("hist_t", [P, 2, COLS])
        cat_rows = sb("cat_rows", [KP, BODY, MOST * P], F16)
        one_hot = sb("one_hot", [KP, 2, KC, MOST * P], BF16)
        w_row = sb("w_row", [P, 2, TILES, H1])
        t1 = sb("t1", [P, 2, M1, COLS])
        t2 = sb("t2", [P, 2, COLS])
        mask_term = sb("mask_term", [P, SLOTS])
        neg_scores = sb("neg_scores", [P, SLOTS])
        neg_max = sb("neg_max", [P, 1])
        exps = sb("exps", [P, SLOTS])
        exp_sum = sb("exp_sum", [P, 1])
        weight_sum = sb("weight_sum", [P, 1])
        inv_sum = sb("inv_sum", [P, 1])
        pool_w = sb("pool_w", [P, TILES, 2, REP // 2])
        pooled_rows = sb("pooled_rows", [P, D])
        pooled_t = sb("pooled_t", [P, 2, B])

        x0 = sb("x0", [P, 4, B])
        spent = hist[:, :, :, :].rearrange("p s u d -> p (s u d)")
        y1 = spent[:, 0:4 * B].rearrange("p (m b) -> p m b", m=4)
        x1 = t1[:, :, :, :].rearrange("p k m b -> p (k m) b")
        spent_w = w_row[:, :, :, :].rearrange("p k r n -> p (k r n)")
        y2 = spent_w[:, 0:2 * B].rearrange("p (m b) -> p m b", m=2)
        x2 = t2
        bn_raw = sb("bn_raw", [P, 10, 6])
        bn_mv = sb("bn_mv", [P, 10, 2])
        eps_col = sb("eps_col", [P, 1])
        bn_mean = sb("bn_mean", [P, 10])
        bn_bs = sb("bn_bs", [P, 10])
        bn_off = sb("bn_off", [P, 10])
        bn_std = sb("bn_std", [P, 10])
        bn_inv = sb("bn_inv", [P, 10])
        bn_scale = sb("bn_scale", [P, 10])
        bn_ms = sb("bn_ms", [P, 10])
        bn_shift = sb("bn_shift", [P, 10])
        half_out = sb("half_out", [P, C, NOUT])
        result = sb("result", [P, C, NOUT])

        cat_slots = [nc.dram_tensor(f"cat_slots{tpr}", [B * tpr, P], F16).ap() for tpr in (1, HALVES)]

        ps_hist = bank("ps_hist")
        ps_z1 = [[bank(f"ps_z1_{k}_{m}") for m in range(M1)] for k in range(2)]
        ps_z2 = bank("ps_z2")
        ps_soft = bank("ps_soft")
        ps_pool = bank("ps_pool")
        ps_out = (ps_pool, ps_soft)

        loaded_own = sem("loaded_own")
        loaded_tok = sem("loaded_tok")
        loaded_mask = sem("loaded_mask")
        loaded_lau = sem("loaded_lau")
        loaded_mlp = sem("loaded_mlp")
        loaded_cat = sem("loaded_cat")
        consts_ready = sem("consts_ready")
        own_idx_ready = sem("own_idx_ready")
        own_gathered = sem("own_gathered")
        user_gathered = sem("user_gathered")
        vec = sem("vec")
        tok_ready = sem("tok_ready")
        flipped = sem("flipped")
        taken = sem("taken")
        setup_done = sem("setup_done")
        params_ready = sem("params_ready")
        most_flipped = sem("most_flipped")
        most_ready = sem("most_ready")
        rest_ready = sem("rest_ready")
        rest_taken = sem("rest_taken")
        counted = sem("counted")
        counts_taken = sem("counts_taken")
        small_ready = sem("small_ready")
        cat_stored = sem("cat_stored")
        parts_ready = sem("parts_ready")
        row_most_ready = sem("row_most_ready")
        halved = sem("halved")
        group_steps = sem("group_steps")
        diag_ready = sem("diag_ready")
        second_flipped = sem("second_flipped")
        second_taken = sem("second_taken")
        rows_known = sem("rows_known")
        cur_ready = sem("cur_ready")
        own_flipped = sem("own_flipped")
        sums_done = sem("sums_done")
        shared_done = sem("shared_done")
        biases_ready = sem("biases_ready")

        idx_copied = sem("idx_copied")
        gathered = [sem(f"gathered{k}") for k in range(BODY)]
        cats_loaded = [sem(f"cats_loaded{k}") for k in range(BODY)]
        one_hot_ready = sem("one_hot_ready")
        cats_done = sem("cats_done")
        cats_taken = sem("cats_taken")
        hist_flipped = sem("hist_flipped")
        hist_taken = sem("hist_taken")
        w_row_ready = sem("w_row_ready")
        z1_done = sem("z1_done")
        t1_ready = sem("t1_ready")
        z2_done = sem("z2_done")
        t2_ready = sem("t2_ready")
        scores_done = sem("scores_done")
        neg_scores_ready = sem("neg_scores_ready")
        mask_term_ready = sem("mask_term_ready")
        exps_ready = sem("exps_ready")
        weight_sum_ready = sem("weight_sum_ready")
        inv_ready = sem("inv_ready")
        exps_flipped = sem("exps_flipped")
        pool_w_ready = sem("pool_w_ready")
        pooled = sem("pooled")
        rows_ready = sem("rows_ready")
        rows_flipped = sem("rows_flipped")
        pooled_taken = sem("pooled_taken")

        own_steps = sem("own_steps")
        user_flipped = sem("user_flipped")
        user_ready = sem("user_ready")
        var_ready = sem("var_ready")
        std_ready = sem("std_ready")
        x0_ready = sem("x0_ready")
        x1_ready = sem("x1_ready")
        x2_ready = sem("x2_ready")
        mlp1_done = sem("mlp1_done")
        mlp2_done = sem("mlp2_done")
        mlp3_done = sem("mlp3_done")
        scale_ready = sem("scale_ready")
        normed = sem("normed")
        result_ready = sem("result_ready")
        stored = sem("stored")

        block = ctx.enter_context(nc.Block())

        ARRIVALS = [16 * (2 * TILES - BY_PRODUCT[j]) for j in range(BODY)]

        def arrived(n, slot):
            turns = n // BODY + 1 if isinstance(n, int) else None
            if turns is not None:
                return ARRIVALS[slot] * turns
            return (n - slot) * (ARRIVALS[slot] // BODY) + ARRIVALS[slot]

        LOADED_MLP = 16 * 15

        def walk(eng, steps, tick, then=None):
            for t in range(PEEL):
                tick(t, t % BODY)
                if then is not None:
                    then(t)
            with eng.Fori(PEEL // BODY, steps // BODY) as i:
                for j in range(BODY):
                    tick(i * BODY + j, j)
            for t in range(steps, steps + LAG):
                tick(t, t % BODY)

        def wait(eng, semaphore, count):
            if not isinstance(count, int) or count > 0:
                eng.wait_ge(semaphore, count)

        def there(n, steps):
            return not isinstance(n, int) or 0 <= n < steps

        def counting(eng, semaphore):
            count = 0

            def chain(ins, more=False):
                nonlocal count
                count += 1
                ins.then_inc(semaphore, 1)
                if not more:
                    eng.wait_ge(semaphore, count)
            return chain

        def spread_loop(sp, tpr):
            steps = B * tpr // TILES

            def tick(n, slot):
                count = BY_PRODUCT[slot]
                wait(sp, one_hot_ready, n - BODY + 1)
                tiles = cat_slots[tpr - 1][bass.ds(n * TILES + TILES - count, count), :]
                sp.dma_start(cat_rows[:, slot, 0:count * P],
                             tiles.rearrange("(a t) s -> a (t s)", a=1).broadcast_to([KP, count * P]))\
                  .then_inc(cats_loaded[slot], 16)

            def store(tok_group):
                group = GROUPS[tok_group]
                sp.wait_ge(small_ready, tok_group + 1)
                sp.dma_start(cat_slots[tpr - 1].rearrange("(c p h) s -> p c (h s)", p=P, h=tpr)[:, group, :],
                             cat_small[:, group, 0:tpr * P]).then_inc(cat_stored, 16)
                sp.wait_ge(cat_stored, 16 * (tok_group + 1))

            store(0)
            for t in range(BODY):
                tick(t, t)
            soon = B // C // TILES // BODY - 1
            for store_first, first, end in ((False, 1, soon), (True, soon, steps // BODY)):
                if store_first:
                    store(1)
                with sp.Fori(first, end) as i:
                    for j in range(BODY):
                        tick(i * BODY + j, j)

        @block.sync
        def _(sp):
            for k, src in enumerate((r_uid, r_mid, r_cat)):
                sp.dma_start(own_raw[:, k, :], src.rearrange("(p c) -> p c", c=C)).then_inc(loaded_own, 16)
            for k, src in enumerate((r_historical_mid, r_historical_cat)):
                sp.dma_start(tok_raw[:, k, :, :], src.rearrange("(p c) t -> p c t", c=C)).then_inc(loaded_tok, 16)
            sp.dma_start(w1_raw[:, :, :], lau_w1.rearrange("(k p) n -> p k n", p=P)).then_inc(loaded_lau, 16)
            sp.dma_start(b1_col[:, :], lau_b1.rearrange("(m p) -> p m", p=P)).then_inc(loaded_lau, 16)
            sp.dma_start(w2_sb[:, :, :], lau_w2.rearrange("(k p) n -> p k n", p=P)).then_inc(loaded_lau, 16)
            sp.dma_start(b2_col[:, :], lau_b2.rearrange("(p a) -> p a", a=1)).then_inc(loaded_lau, 16)
            sp.dma_start(w3_sb[:, :], lau_w3).then_inc(loaded_lau, 16)
            sp.dma_start(b3_all[:, :],
                         lau_b3.rearrange("(a n) -> a n", a=1).broadcast_to([P, 1])).then_inc(loaded_lau, 16)
            for k, src in enumerate((bn0_g, bn0_b)):
                sp.dma_start(bn0[0:E, k, 0:1], src[0:E].rearrange("(p a) -> p a", a=1)).then_inc(loaded_mlp, 16)
                sp.dma_start(bn0[:, k, 1:4], src[E:].rearrange("(c p) -> p c", p=P)).then_inc(loaded_mlp, 16)
            sp.dma_start(cat_f[:, :, :], cat_table.rearrange("(k p) e -> p k e", p=KP)).then_inc(loaded_cat, 16)
            for k, (g1, g2) in enumerate(((bn1_g, bn2_g), (bn1_b, bn2_b))):
                sp.dma_start(bn1[:, k, :], g1.rearrange("(c p) -> p c", p=P)).then_inc(loaded_mlp, 16)
                sp.dma_start(bn2[:, k, :], g2.rearrange("(c p) -> p c", p=P)).then_inc(loaded_mlp, 16)
            sp.dma_start(mw1[0:E, 0, :], mlp_w1[0:E, :]).then_inc(loaded_mlp, 16)
            sp.dma_start(mw1[:, 1:4, :], mlp_w1[E:, :].rearrange("(c p) n -> p c n", p=P)).then_inc(loaded_mlp, 16)
            sp.dma_start(mb1[:, :], mlp_b1.rearrange("(m p) -> p m", p=P)).then_inc(loaded_mlp, 16)
            sp.dma_start(mw2[:, :, :], mlp_w2.rearrange("(k p) n -> p k n", p=P)).then_inc(loaded_mlp, 16)
            sp.dma_start(mb2[:, :], mlp_b2.rearrange("(m p) -> p m", p=P)).then_inc(loaded_mlp, 16)
            sp.dma_start(mw3[:, :, :], mlp_w3.rearrange("(k p) n -> p k n", p=P)).then_inc(loaded_mlp, 16)
            sp.dma_start(mb3[:, :],
                         mlp_b3.rearrange("(a n) -> a n", a=1).broadcast_to([P, NOUT])).then_inc(loaded_mlp, 16)
            sp.wait_ge(most_ready, 1)
            with sp.If(sp.value_load(most[0:1, 0:1], min_val=0, max_val=T) > P):
                spread_loop(sp, HALVES)
            with sp.Else():
                spread_loop(sp, 1)
            sp.wait_ge(result_ready, 1)
            sp.dma_start(out.rearrange("(p c) n -> p c n", c=C), result[:, :, :]).then_inc(stored, 16)
            sp.wait_ge(stored, 16)

        def gather(pool, dst, table, idx, done):
            pool.indirect_dma_start(dst, None, table[:, :],
                                    bass.IndirectOffsetOnAxis(idx, axis=0)).then_inc(done, 16)

        def gather_loop(pool, tpr):
            rows = TILES // tpr
            steps = B // rows

            def tick(n, slot):
                wait(pool, pooled, n - BODY + 1)
                wait(pool, idx_copied, n + 1)
                pool.nop(nofuse=True)
                for u in range(TILES):
                    r, h = divmod(u, tpr)
                    at = h * rows + r
                    gather(pool, hist[:, slot, u, 0:E], mat_table, idx_ring[:, slot, 0, at:at + 1], gathered[slot])
                    if u >= TILES - BY_PRODUCT[slot]:
                        continue
                    gather(pool, hist[:, slot, u, E:D], cat_table, idx_ring[:, slot, 1, at:at + 1], gathered[slot])

            for t in range(BODY):
                tick(t, t)
            with pool.Fori(1, steps // BODY) as i:
                for j in range(BODY):
                    tick(i * BODY + j, j)

        @block.gpsimd
        def _(pool):
            pool.memset(ident[:, :], 0.0).then_inc(consts_ready, 1)
            pool.memset(ones[:, :], 1.0).then_inc(consts_ready, 1)
            pool.memset(ones_t[:, :], 1.0)
            pool.memset(eps_col[:, :], EPS)
            pool.memset(tok[:, :, :, T:SLOTS], 0.0).then_inc(consts_ready, 1)
            pool.iota(ramp[:, :], [[1, SLOTS]], base=0, channel_multiplier=0,
                      allow_small_or_imprecise_dtypes=True).then_inc(consts_ready, 1)
            pool.iota(ramp_1[:, :], [[1, T]], base=1, channel_multiplier=0,
                      allow_small_or_imprecise_dtypes=True)
            pool.iota(part_id[:, :], [[1, 1]], base=0, channel_multiplier=1).then_inc(consts_ready, 1)
            pool.iota(cat_id[:, :], [[KP, KC]], base=0, channel_multiplier=1,
                      allow_small_or_imprecise_dtypes=True).then_inc(consts_ready, 1)
            pool.wait_ge(consts_ready, 6)
            pool.affine_select(out=ident[:, :], in_=ident[:, :], compare_op=ALU.not_equal, fill=1.0,
                               base=0, pattern=[[-1, P]], channel_multiplier=1).then_inc(consts_ready, 1)
            pool.wait_ge(own_idx_ready, 3)
            for c in range(C):
                gather(pool, own_tok[:, c, 0:E], mat_table, own_idx[:, 1, c:c + 1], own_gathered)
                gather(pool, own_tok[:, c, E:D], cat_table, own_idx[:, 2, c:c + 1], own_gathered)
            for c in range(C):
                gather(pool, user_tok[:, c, :], user_table, own_idx[:, 0, c:c + 1], user_gathered)
            pool.wait_ge(loaded_lau, 96)
            pool.tensor_tensor(w_cur[:, :], w1_raw[:, 0, :], w1_raw[:, 2, :], ALU.add).then_inc(params_ready, 1)
            pool.tensor_tensor(w_base[:, :], w1_raw[:, 1, :], w1_raw[:, 2, :], ALU.subtract).then_inc(params_ready, 1)
            pool.wait_ge(row_most_ready, 1)
            pool.wait_ge(consts_ready, 7)
            for c in range(C):
                pool.tensor_scalar(count_diag[:, c, :], ident[:, :], place[:, c, T - 1:T], None,
                                   ALU.mult).then_inc(diag_ready, 1)
            pool.wait_ge(most_ready, 1)
            with pool.If(pool.value_load(most[0:1, 0:1], min_val=0, max_val=T) > P):
                gather_loop(pool, HALVES)
            with pool.Else():
                gather_loop(pool, 1)

        def mlp1(pe, m, chunks):
            for k in chunks:
                size = CHUNKS[k][1]
                last = pe.matmul(ps_z1[m // 2][m % 2][:, :], mw1[0:size, k, m * P:(m + 1) * P],
                                 x0[0:size, k, :], start=(k == 0), stop=(k == 3))
            return last

        def tensor_loop(pe, tpr):
            rows = TILES // tpr
            width = tpr * P
            steps = B // rows
            parts = rows * REP
            scores = ps_soft[0:parts, 0:width]
            exp_cols = ps_pool[:, 0:tpr * parts]
            pool_rows = ps_pool[0:parts, 128:128 + D]
            pool_cols = ps_pool[:, 256:256 + parts]

            def tick(t, j):
                n, k = t - 2, (j - 2) % 2
                if there(n, steps):
                    wait(pe, hist_taken, n + 1)
                    wait(pe, w_row_ready, n + 1)
                    wait(pe, t1_ready, M1 * (n - 1))
                    for m in range(M1):
                        for r in range(rows):
                            last = pe.matmul(ps_z1[k][m][:, r * width:(r + 1) * width],
                                             w_row[:, k, r, m * P:(m + 1) * P],
                                             hist_t[:, k, r * width:(r + 1) * width], start=True, stop=True)
                        last.then_inc(z1_done, 1)
                n = t - 5
                if there(n, steps):
                    wait(pe, exps_ready, n + 1)
                    wait(pe, pooled_taken, n)
                    if parts < P:
                        pe.nop(nofuse=True)
                    for h in range(tpr):
                        last = pe.transpose(exp_cols[:, h * parts:(h + 1) * parts],
                                            exps[0:parts, h * P:(h + 1) * P], ident[0:parts, 0:parts])
                    last.then_inc(exps_flipped, 1)
                n, k = t - 4, (j - 4) % 2
                if there(n, steps):
                    wait(pe, t2_ready, n + 1)
                    wait(pe, neg_scores_ready, n)
                    for h in range(tpr):
                        for r in range(rows):
                            at = (r * tpr + h) * P
                            last = pe.matmul(scores[r * REP:(r + 1) * REP, h * P:(h + 1) * P], w3_half[:, 0:REP],
                                             t2[:, k, at:at + P], start=True, stop=True)
                    last.then_inc(scores_done, 1)
                n, slot = t - 1, (j - 1) % BODY
                if there(n, steps):
                    wait(pe, gathered[slot], arrived(n, slot))
                    wait(pe, cats_taken, n + 1)
                    for u in range(TILES):
                        last = pe.transpose(ps_hist[:, u * P:(u + 1) * P], hist[:, slot, u, :], ident[:, :])
                    last.then_inc(hist_flipped, 1)
                n, slot = t - 5, (j - 5) % BODY
                if there(n, steps):
                    wait(pe, pool_w_ready, n + 1)
                    for r in range(rows):
                        for h in range(tpr):
                            last = pe.matmul(pool_rows[r * REP:(r + 1) * REP, :],
                                             pool_w[:, h * rows + r, :, :].rearrange("p k i -> p (k i)"),
                                             hist[:, slot, r * tpr + h, :], start=(h == 0), stop=(h == tpr - 1))
                    last.then_inc(pooled, 1)
                n, k = t - 3, (j - 3) % 2
                if there(n, steps):
                    wait(pe, t1_ready, M1 * (n + 1))
                    if isinstance(n, int) and n == 0:
                        wait(pe, counts_taken, 2 * rows)
                    wait(pe, t2_ready, n)
                    for m in range(M1):
                        last = pe.matmul(ps_z2[:, :], w2_sb[:, m, :], t1[:, k, m, :],
                                         start=(m == 0), stop=(m == M1 - 1))
                    last.then_inc(z2_done, 1)
                n = t - 5
                if there(n, steps):
                    wait(pe, rows_ready, n + 1)
                    if parts < P:
                        pe.nop(nofuse=True)
                    pe.transpose(pool_cols, pooled_rows[0:parts, :], ident[0:parts, 0:parts]).then_inc(rows_flipped, 1)
                n, k, count = t, j % 2, BY_PRODUCT[j]
                if there(n, steps):
                    wait(pe, one_hot_ready, n + 1)
                    wait(pe, hist_taken, n)
                    for u in range(count):
                        for chunk in range(KC):
                            last = pe.matmul(ps_hist[:, u * 3 * E:(u + 1) * 3 * E],
                                             one_hot[:, k, chunk, u * P:(u + 1) * P],
                                             cat_part[:, chunk, :, :].rearrange("p a e -> p (a e)"),
                                             start=(chunk == 0), stop=(chunk == KC - 1))
                    last.then_inc(cats_done, 1)
                early = {steps + 2: range(0, 2), steps + 3: range(2, 3), steps + 4: range(3, 4)}
                if isinstance(t, int) and t in early:
                    pe.wait_ge(x0_ready, 2)
                    pe.wait_ge(t1_ready, M1 * steps)
                    pe.wait_ge(loaded_mlp, LOADED_MLP)
                    for m in early[t]:
                        mlp1(pe, m, range(0, 2))

            def then(t):
                if t < PEEL - 1:
                    return
                pe.wait_ge(tok_ready, 2)
                pe.wait_ge(t1_ready, M1 * (PEEL - 3))
                for q in range(3 * tpr):
                    h, k = divmod(q, 3)
                    if q >= M1:
                        pe.wait_ge(rest_taken, q - M1 + 1)
                    for c in range(1, C):
                        last = pe.transpose(ps_z1[0][q % M1][:, (c - 1) * P:c * P], tok[:, k, c, h * P:(h + 1) * P],
                                            ident[:, :])
                    last.then_inc(rest_ready, 1)
                pe.wait_ge(rest_taken, 3 * tpr)

            walk(pe, steps, tick, then)

        @block.tensor
        def _(pe):
            pe.wait_ge(consts_ready, 7)
            pe.wait_ge(row_most_ready, 1)
            pe.transpose(ps_soft[0:1, 0:P], row_most[:, :], ident[:, :]).then_inc(most_flipped, 1)
            pe.wait_ge(loaded_lau, 96)
            pe.wait_ge(halved, 4)
            for m in range(M1):
                pe.matmul(ps_z2[:, 0:1], w2_sb[:, m, :], ones[:, 0:1], start=(m == 0), stop=(m == M1 - 1))
            pe.matmul(ps_z2[:, 1:2], w3_half[:, :], ones[:, 0:1], start=True, stop=True).then_inc(sums_done, 1)
            pe.wait_ge(own_gathered, 16 * 2 * C)
            for c in range(C):
                last = pe.transpose(ps_hist[:, c * P:(c + 1) * P], own_tok[:, c, :], ident[:, :])
            last.then_inc(own_flipped, 1)
            pe.wait_ge(cur_ready, 1)
            pe.wait_ge(params_ready, 1)
            for m in range(M1):
                last = pe.matmul(ps_z1[1][m][:, :], w_cur[:, m * P:(m + 1) * P], cur_t[:, :], start=True, stop=True)
                last.then_inc(shared_done, 1)
            pe.wait_ge(user_gathered, 16 * C)
            pe.wait_ge(cur_ready, 1)
            for c in range(C):
                last = pe.transpose(ps_hist[0:E, c * P:(c + 1) * P], user_tok[:, c, :], ident[:, :])
            last.then_inc(user_flipped, 1)
            pe.wait_ge(tok_ready, 1)
            for k in range(3):
                last = pe.transpose(ps_z1[0][0][:, k * P:(k + 1) * P], tok[:, k, 0, 0:P], ident[:, :])
            last.then_inc(flipped, 1)
            pe.wait_ge(setup_done, M1)
            pe.wait_ge(taken, 2)
            pe.wait_ge(biases_ready, 2)
            pe.wait_ge(diag_ready, C)
            pe.matmul(ps_z2[:, :], ones[:, :], count_diag[:, :, :].rearrange("p c q -> p (c q)"),
                      start=True, stop=True).then_inc(counted, 1)
            pe.wait_ge(parts_ready, 1)
            pe.wait_ge(user_ready, 1)
            pe.wait_ge(most_ready, 1)
            with pe.If(pe.value_load(most[0:1, 0:1], min_val=0, max_val=T) > P):
                for k in range(3):
                    last = pe.transpose(ps_z1[0][1][:, k * P:(k + 1) * P], tok[:, k, 0, P:SLOTS], ident[:, :])
                last.then_inc(second_flipped, 1)
                pe.wait_ge(second_taken, 2)
                tensor_loop(pe, HALVES)
            with pe.Else():
                tensor_loop(pe, 1)
            pe.wait_ge(x0_ready, 3)
            mlp1(pe, 0, (2,))
            pe.wait_ge(x0_ready, 4)
            mlp1(pe, 0, (3,)).then_inc(mlp1_done, 1)
            for m in range(1, 4):
                mlp1(pe, m, range(2, 4)).then_inc(mlp1_done, 1)
            for k in range(4):
                pe.wait_ge(x1_ready, k + 1)
                for m in range(2):
                    last = pe.matmul((ps_z2, ps_hist)[m][:, :], mw2[:, k, m * P:(m + 1) * P], x1[:, k, :],
                                     start=(k == 0), stop=(k == 3))
                    if k == 3:
                        last.then_inc(mlp2_done, 1)
            for k in range(2):
                pe.wait_ge(x2_ready, k + 1)
                for c in range(C):
                    last = pe.matmul(ps_out[k][:, c * NOUT:(c + 1) * NOUT], x2[:, k, c * P:(c + 1) * P], mw3[:, k, :],
                                     start=True, stop=True)
                last.then_inc(mlp3_done, 1)

        def std(act, first, count, turn):
            cols = slice(first, first + count)
            act.wait_ge(var_ready, turn)
            act.activation(bn_std[:, cols], bn_mv[:, cols, 1], ACT.Sqrt, bias=eps_col[:, :]).then_inc(std_ready, 1)

        def scalar_loop(act, tpr):
            rows = TILES // tpr
            width = tpr * P
            parts = rows * REP
            steps = B // rows

            def copy_idx(n, slot):
                wait(act, gathered[slot], arrived(n, slot) - ARRIVALS[slot])
                view = idx_ring[:, slot, :, :].rearrange("p k (h r) -> p k h r", h=tpr)
                act.activation(view, slot_idx[:, :, 0:tpr, bass.ds(n * rows, rows)], ACT.Copy).then_inc(idx_copied, 1)

            def tick(t, j):
                if not isinstance(t, int) or t < steps:
                    copy_idx(t + AHEAD, (j + AHEAD) % BODY)
                if isinstance(t, int) and t == 1:
                    std(act, 0, 2, 1)
                n, k = t - 2, (j - 2) % 2
                if there(n, steps):
                    wait(act, z2_done, n - 1)
                    for m in range(M1):
                        wait(act, z1_done, M1 * n + m + 1)
                        for r in range(rows):
                            last = act.activation(t1[:, k, m, r * width:(r + 1) * width],
                                                  ps_z1[k][m][:, r * width:(r + 1) * width], ACT.Tanh,
                                                  bias=z1_bias[:, m, bass.ds(n * rows + r, 1)], scale=0.5)
                        last.then_inc(t1_ready, 1)
                n, k = t - 1, (j - 1) % 2
                if there(n, steps):
                    wait(act, hist_flipped, n + 1)
                    wait(act, z1_done, M1 * (n - 1))
                    act.activation(hist_t[:, k, :], ps_hist[:, :], ACT.Copy).then_inc(hist_taken, 1)
                n = t - 4
                if there(n, steps):
                    wait(act, neg_scores_ready, n + 1)
                    wait(act, exps_flipped, n)
                    wait(act, weight_sum_ready, n)
                    act.activation(exps[0:parts, 0:width], neg_scores[0:parts, 0:width], ACT.Exp, scale=-1.0,
                                   bias=neg_max[0:parts, :], accum_out=exp_sum[0:parts, :]).then_inc(exps_ready, 1)
                n = t - 5
                if there(n, steps):
                    wait(act, inv_ready, n + 1)
                    wait(act, pooled, n + 1)
                    wait(act, rows_flipped, n)
                    act.activation(pooled_rows[0:parts, :], ps_pool[0:parts, 128:128 + D], ACT.Copy,
                                   scale=inv_sum[0:parts, :]).then_inc(rows_ready, 1)
                n, k = t - 3, (j - 3) % 2
                if there(n, steps):
                    wait(act, z2_done, n + 1)
                    wait(act, scores_done, n - 1)
                    act.activation(t2[:, k, :], ps_z2[:, :], ACT.Tanh, bias=z2_bias[:, :],
                                   scale=0.25).then_inc(t2_ready, 1)
                n = t - 5
                if there(n, steps):
                    wait(act, rows_flipped, n + 1)
                    cols = ps_pool[:, 256:256 + parts].rearrange("p (r k i) -> p k r i", r=rows, k=2)
                    act.activation(pooled_t[:, :, bass.ds(n * rows, rows)], cols[:, :, :, 0],
                                   ACT.Copy).then_inc(pooled_taken, 1)

            if tpr == 1:
                act.wait_ge(taken, 2)
            else:
                act.wait_ge(second_taken, 2)
            for n in range(AHEAD):
                copy_idx(n, n)
            wait(act, counted, 1)
            for r in range(rows):
                quad = slice(r * REP, (r + 1) * REP)
                counts = ps_z2[quad, :].rearrange("p (n r) -> p r n", r=rows)[:, r, :]
                act.activation(count_level[quad, 0:steps], counts, ACT.Copy, scale=BIG).then_inc(counts_taken, 1)
                act.activation(count_mean[quad, 0:steps], counts, ACT.Copy, scale=for_mean[quad, :])\
                   .then_inc(counts_taken, 1)
            def then(t):
                if t < PEEL - 1:
                    return
                for q in range(3 * tpr):
                    h, k = divmod(q, 3)
                    act.wait_ge(rest_ready, q + 1)
                    act.activation(slot_idx[:, k, h, P:B] if k < 2 else slot_mask[:, h, P:B],
                                   ps_z1[0][q % M1][:, 0:B - P], ACT.Copy).then_inc(rest_taken, 1)
                act.wait_ge(rest_taken, 3 * tpr)

            walk(act, steps, tick, then)

        @block.scalar
        def _(act):
            act.dma_start(tok_raw[:, 2, :, :], r_mask.rearrange("(p c) t -> p c t", c=C)).then_inc(loaded_mask, 16)
            act.wait_ge(loaded_lau, 96)
            act.activation(w3_col[:, :], w3_sb[:, :], ACT.Copy, scale=0.5).then_inc(halved, 1)
            act.activation(b1_half[:, :], b1_col[:, :], ACT.Copy, scale=0.5).then_inc(halved, 1)
            act.activation(b2_half[:, :], b2_col[:, :], ACT.Copy, scale=0.5).then_inc(halved, 1)
            act.wait_ge(halved, 3)
            act.wait_ge(consts_ready, 6)
            act.activation(w3_half[:, :], ones[:, :], ACT.Copy, scale=w3_col[:, :]).then_inc(halved, 1)
            act.wait_ge(sums_done, 1)
            act.activation(z2_bias[:, :], ps_z2[:, 0:1], ACT.Identity, scale=0.25,
                           bias=b2_half[:, :]).then_inc(biases_ready, 1)
            act.activation(score_bias[:, :], ps_z2[:, 1:2], ACT.Identity, bias=b3_all[:, :]).then_inc(biases_ready, 1)
            act.wait_ge(own_flipped, 1)
            act.activation(cur_t[:, :], ps_hist[:, :], ACT.Copy).then_inc(cur_ready, 1)
            for m in range(M1):
                act.wait_ge(shared_done, 1 + m)
                act.activation(z1_bias[:, m, :], ps_z1[1][m][:, :], ACT.Identity, scale=0.5,
                               bias=b1_half[:, m:m + 1]).then_inc(setup_done, 1)
            act.wait_ge(user_flipped, 1)
            act.activation(user_t[0:E, :], ps_hist[0:E, :], ACT.Copy).then_inc(user_ready, 1)
            act.wait_ge(setup_done, M1)
            act.wait_ge(biases_ready, 2)
            act.wait_ge(rows_known, 2)
            act.wait_ge(most_ready, 1)
            with act.If(act.value_load(most[0:1, 0:1], min_val=0, max_val=T) > P):
                scalar_loop(act, HALVES)
            with act.Else():
                scalar_loop(act, 1)

            def scaled(turn, first, outs, banks):
                act.wait_ge(scale_ready, turn)
                for k, (y, ps) in enumerate(zip(outs, banks)):
                    act.activation(y, ps[:, :], ACT.Identity, scale=bn_scale[:, first + k:first + k + 1],
                                   bias=bn_off[:, first + k:first + k + 1]).then_inc(normed, 1)

            std(act, 2, 2, 2)
            for half in range(2):
                ms = (2 * half, 2 * half + 1)
                std(act, 4 + ms[0], 2, 3 + half)
                scaled(1 + half, 4 + ms[0], [y1[:, m, :] for m in ms], [ps_z1[half][m % 2] for m in ms])
            for m in range(2):
                std(act, 8 + m, 1, 5 + m)
                scaled(3 + m, 8 + m, [y2[:, m, :]], [(ps_z2, ps_hist)[m]])

        def moments(dve, chain, first, sources, done=None, turn=0):
            for k, x in enumerate(sources):
                if done is not None:
                    dve.wait_ge(done, turn + k + 1)
                chain(dve.bn_stats(bn_raw[:, first + k, :], x), k < len(sources) - 1)
            for k in range(len(sources)):
                last = dve.bn_aggr(bn_mv[:, first + k, :], bn_raw[:, first + k, :])
            last.then_inc(var_ready, 1)
            dve.wait_ge(var_ready, MOMENTS.index(first) + 1)

        def gains(dve, chain, first, count, affine, own, bias=None):
            cols, these = slice(first, first + count), slice(own, own + count)
            mean = bn_mv[:, cols, 0]
            if bias is not None:
                chain(dve.tensor_tensor(bn_mean[:, cols], bn_mv[:, cols, 0], bias[:, these], ALU.add))
                mean = bn_mean[:, cols]
            dve.wait_ge(std_ready, MOMENTS.index(first) + 1)
            chain(dve.reciprocal(bn_inv[:, cols], bn_std[:, cols]))
            chain(dve.tensor_tensor(bn_scale[:, cols], bn_inv[:, cols], affine[:, 0, these], ALU.mult))
            chain(dve.tensor_tensor(bn_ms[:, cols], mean, bn_scale[:, cols], ALU.mult), bias is not None)
            if bias is not None:
                chain(dve.tensor_tensor(bn_bs[:, cols], bias[:, these], bn_scale[:, cols], ALU.mult))
            chain(dve.tensor_tensor(bn_shift[:, cols], affine[:, 1, these], bn_ms[:, cols], ALU.subtract))
            if bias is not None:
                dve.tensor_tensor(bn_off[:, cols], bn_shift[:, cols], bn_bs[:, cols], ALU.add).then_inc(scale_ready, 1)

        MOMENTS = (0, 2, 4, 6, 8, 9)

        def norm_inputs(dve, chain, first, sources):
            gains(dve, chain, first, 2, bn0, first)
            for k, x in enumerate(sources, first):
                dve.tensor_scalar(x0[:, k, :], x, bn_scale[:, k:k + 1], bn_shift[:, k:k + 1],
                                  ALU.mult, ALU.add).then_inc(x0_ready, 1)
        BITS = (T - 1).bit_length()
        doubles = (2, 3, PEEL - 4, PEEL - 3)
        HALF_SHIFTS = [[] for _ in range(PEEL)]
        for half in range(2 * BITS):
            HALF_SHIFTS[next(t for t in range(2, PEEL - 2) if len(HALF_SHIFTS[t]) < 1 + (t in doubles))].append(half)

        def prepare(dve, chain, tok_group):
            group = GROUPS[tok_group]
            for k, size in enumerate((NM, NC)):
                chain(dve.tensor_scalar(tok_wrap[:, k, group, :], tok_raw[:, k, group, :], 0, size,
                                        ALU.is_lt, ALU.mult), True)
                chain(dve.tensor_scalar(tok_clip[:, k, group, :], tok_raw[:, k, group, :], -size, size - 1,
                                        ALU.max, ALU.min), True)
            for c in range(group.start, group.stop):
                chain(dve.tensor_scalar(tok[:, 2, c, :], ramp[:, :], place[:, c, T - 1:T], None, ALU.is_lt), True)
            for c in range(group.start, group.stop):
                chain(dve.tensor_tensor(gap[:, c, :], ramp_1[:, :], place[:, c, :], ALU.subtract),
                      c < group.stop - 1)

        def start_group(dve, chain, tok_group):
            group = GROUPS[tok_group]
            for k in range(2):
                chain(dve.tensor_tensor(tok_int[:, k, group, :], tok_clip[:, k, group, :],
                                        tok_wrap[:, k, group, :], ALU.add), True)
            chain(dve.tensor_tensor(shift[:, 0, group, :], gap[:, group, :], mask_f[:, group, :], ALU.mult))
            chain(dve.scalar_tensor_tensor(out=key[:, 0, group, :], in0=tok_int[:, 0, group, :], scalar=CAT_BITS,
                                           in1=tok_int[:, 1, group, :], op0=ALU.logical_shift_left,
                                           op1=ALU.bitwise_or))

        def shift_group(dve, chain, tok_group, bit, halves=range(2)):
            group = GROUPS[tok_group]
            at = (slice(None), group)
            by, old, new = 1 << bit, bit % 2, 1 - bit % 2
            if 0 in halves:
                chain(dve.tensor_scalar(moving[at], shift[:, old, group, :], by, None, ALU.bitwise_and), True)
                chain(dve.tensor_copy(key[:, new, group, :], key[:, old, group, :]))
                chain(dve.scalar_tensor_tensor(out=shift[:, new, group, :], in0=moving[at], scalar=0,
                                               in1=shift[:, old, group, :], op0=ALU.is_equal, op1=ALU.mult))
            if 1 in halves:
                chain(dve.copy_predicated(key[:, new, group, 0:T - by], moving[:, group, by:T],
                                          key[:, old, group, by:T]), True)
                chain(dve.copy_predicated(shift[:, new, group, 0:T - by], moving[:, group, by:T],
                                          shift[:, old, group, by:T]))

        def end_group(dve, chain, tok_group):
            group = GROUPS[tok_group]
            end = BITS % 2
            chain(dve.tensor_single_scalar(part[:, 0, group, :], key[:, end, group, :], CAT_BITS,
                                           ALU.logical_shift_right), True)
            chain(dve.tensor_single_scalar(part[:, 1, group, :], key[:, end, group, :], (1 << CAT_BITS) - 1,
                                           ALU.bitwise_and))
            for k in range(2):
                last = dve.tensor_copy(tok[:, k, group, 0:T], part[:, k, group, :])
            last.then_inc(tok_ready, 1)
            dve.wait_ge(tok_ready, tok_group + 1)
            dve.tensor_copy(cat_small[:, group, :], tok[:, 1, group, :]).then_inc(small_ready, 1)

        def vector_loop(dve, tpr):
            rows = TILES // tpr
            width = tpr * P
            parts = rows * REP
            steps = B // rows

            own_chain = counting(dve, own_steps)

            def one_hots(k, slot, count, chunks):
                for chunk in chunks:
                    last = dve.tensor_scalar(one_hot[:, k, chunk, 0:count * P], cat_rows[:, slot, 0:count * P],
                                             cat_id[0:KP, chunk:chunk + 1], None, ALU.is_equal)
                return last

            def tick(t, j):
                n, slot = t - 1, (j - 1) % BODY
                count = BY_PRODUCT[slot]
                if there(n, steps):
                    wait(dve, cats_done, n + 1)
                    wait(dve, pooled, n - BODY + 1)
                    dve.tensor_reduce(hist[:, slot, TILES - count:TILES, E:D],
                                      ps_hist[:, 0:count * 3 * E].rearrange("p (u a e) -> p u e a", a=3, e=E),
                                      AX.X, ALU.add).then_inc(cats_taken, 1)
                n = t - 5
                if there(n, steps):
                    wait(dve, exps_ready, n + 1)
                    dve.scalar_tensor_tensor(out=weight_sum[0:parts, :], in0=exp_sum[0:parts, :],
                                             scalar=for_probs[0:parts, :], in1=count_mean[0:parts, bass.ds(n, 1)],
                                             op0=ALU.mult, op1=ALU.add).then_inc(weight_sum_ready, 1)
                    wait(dve, weight_sum_ready, n + 1)
                    wait(dve, rows_ready, n)
                    dve.reciprocal(inv_sum[0:parts, :], weight_sum[0:parts, :]).then_inc(inv_ready, 1)
                n, k, slot, count = t, j % 2, j, BY_PRODUCT[j]
                if there(n, steps):
                    wait(dve, cats_done, n - 1)
                    wait(dve, cats_loaded[slot],
                         16 * (n // BODY + 1) if isinstance(n, int) else (n - slot) * (16 // BODY) + 16)
                    one_hots(k, slot, count, FIRST_CHUNKS)
                n = t - 5
                if there(n, steps):
                    wait(dve, exps_flipped, n + 1)
                    wait(dve, pooled, n)
                    mask = slot_mask[:, 0:tpr, bass.ds(n * rows, rows)].rearrange(
                        "p h (r i) -> p h r i", i=1).broadcast_to([P, tpr, rows, REP // 2])
                    weights = pool_w[:, :, :, :].rearrange("p (h r) k i -> p k h r i", h=tpr)
                    exp_cols = ps_pool[:, 0:tpr * parts].rearrange("p (h r k i) -> p k h r i", h=tpr, r=rows, k=2)
                    dve.tensor_tensor(weights[:, 0, :, :, :], exp_cols[:, 0, :, :, :], mask, ALU.mult)
                    dve.tensor_copy(weights[:, 1, :, :, :], mask).then_inc(pool_w_ready, 1)
                if there(t, steps):
                    one_hots(j % 2, j, BY_PRODUCT[j], LAST_CHUNKS).then_inc(one_hot_ready, 1)
                if isinstance(t, int) and t == 0:
                    dve.wait_ge(user_ready, 1)
                    moments(dve, own_chain, 0, [user_t[:, :], cur_t[:, :]])
                if isinstance(t, int) and t == 2:
                    dve.wait_ge(loaded_mlp, LOADED_MLP)
                    norm_inputs(dve, own_chain, 0, [user_t[:, :], cur_t[:, :]])
                n = t - 4
                if there(n, steps):
                    if isinstance(n, int) and n == 0:
                        wait(dve, counts_taken, 2 * rows)
                    wait(dve, scores_done, n + 1)
                    wait(dve, exps_ready, n)
                    dve.tensor_scalar(mask_term[0:parts, 0:width], slot_level[0:parts, 0:width],
                                      count_level[0:parts, bass.ds(n, 1)], score_bias[0:parts, :],
                                      ALU.add, ALU.min).then_inc(mask_term_ready, 1)
                    wait(dve, mask_term_ready, n + 1)
                    dve.nop(nofuse=True)
                    dve.tensor_tensor_reduce(out=neg_scores[0:parts, 0:width], in0=ps_soft[0:parts, 0:width],
                                             in1=mask_term[0:parts, 0:width], scale=-1.0, scalar=3e38,
                                             op0=ALU.add, op1=ALU.min,
                                             accum_out=neg_max[0:parts, :]).then_inc(neg_scores_ready, 1)
                n, k = t - 1, (j - 1) % 2
                if there(n, steps):
                    wait(dve, z1_done, M1 * (n - 1))
                    for r in range(rows):
                        last = dve.scalar_tensor_tensor(out=w_row[:, k, r, :], in0=w_prod,
                                                        scalar=cur_t[:, bass.ds(n * rows + r, 1)],
                                                        in1=w_base[:, :], op0=ALU.mult, op1=ALU.add)
                    last.then_inc(w_row_ready, 1)

            group_chain = counting(dve, group_steps)

            def then(t):
                if t == 0:
                    prepare(dve, group_chain, 1)
                if t == 1:
                    start_group(dve, group_chain, 1)
                for half in HALF_SHIFTS[t]:
                    shift_group(dve, group_chain, 1, half // 2, (half % 2,))
                if t == PEEL - 2:
                    end_group(dve, group_chain, 1)
                if t == PEEL - 1:
                    dve.wait_ge(rest_taken, 3 * tpr)

            walk(dve, steps, tick, then)
            dve.wait_ge(pooled_taken, steps)

        @block.vector
        def _(dve):
            chain = counting(dve, vec)
            chain(dve.memset(user_t[E:P, :], 0.0), True)
            chain(dve.memset(bn0[E:P, :, 0:1], 0.0), True)
            chain(dve.memset(slot_idx[:, :, :, B:], 0), True)
            dve.wait_ge(consts_ready, 6)
            chain(dve.tensor_single_scalar(upper[:, :], part_id[:, :], REP // 2, ALU.bitwise_and))
            dve.tensor_scalar(for_probs[:, :], upper[:, :], 0, None, ALU.is_equal).then_inc(rows_known, 1)
            dve.tensor_scalar(for_mean[:, :], upper[:, :], 0, None, ALU.not_equal).then_inc(rows_known, 1)
            dve.tensor_scalar(slot_level[:, :], ramp[:, :], 0.5, -BIG, ALU.add, ALU.mult).then_inc(rows_known, 1)
            dve.wait_ge(loaded_own, 48)
            for k, size in enumerate((NU, NM, NC)):
                chain(dve.tensor_scalar(own_wrap[:, k, :], own_raw[:, k, :], 0, size, ALU.is_lt, ALU.mult), k < 2)
            chain(dve.tensor_tensor(own_sum[:, :, :], own_wrap[:, :, :], own_raw[:, :, :], ALU.add))
            for k, size in enumerate((NU, NM, NC)):
                dve.tensor_scalar(own_idx[:, k, :], own_sum[:, k, :], 0, size - 1,
                                  ALU.max, ALU.min).then_inc(own_idx_ready, 1)
            dve.wait_ge(loaded_mask, 16)
            chain(dve.tensor_copy(mask_f[:, :, :], tok_raw[:, 2, :, :]))
            for c in range(C):
                chain(dve.tensor_tensor_scan(place[:, c, :], ones_t[:, :], mask_f[:, c, :], 0.0,
                                             ALU.mult, ALU.add), c < C - 1)
            dve.tensor_reduce(row_most[:, :], place[:, :, T - 1], AX.X, ALU.max).then_inc(row_most_ready, 1)

            dve.wait_ge(loaded_tok, 32)
            prepare(dve, chain, 0)
            start_group(dve, chain, 0)
            for bit in range(BITS):
                shift_group(dve, chain, 0, bit)
            end_group(dve, chain, 0)
            dve.wait_ge(most_flipped, 1)
            chain(dve.tensor_reduce(most[:, :], ps_soft[0:1, 0:P], AX.X, ALU.max))
            dve.sem_inc(most_ready, 1)
            dve.wait_ge(flipped, 1)
            dve.tensor_copy(slot_idx[:, :, 0, 0:P],
                            ps_z1[0][0][:, 0:2 * P].rearrange("p (k b) -> p k b", k=2)).then_inc(taken, 1)
            dve.tensor_copy(slot_mask[:, 0, 0:P], ps_z1[0][0][:, 2 * P:3 * P]).then_inc(taken, 1)
            dve.wait_ge(loaded_cat, 16)
            chain(dve.tensor_copy(cat_part[:, :, 0, :], cat_f[:, :, :]))
            chain(dve.tensor_tensor(cat_rest[:, 0, :, :], cat_f[:, :, :], cat_part[:, :, 0, :], ALU.subtract))
            chain(dve.tensor_copy(cat_part[:, :, 1, :], cat_rest[:, 0, :, :]))
            chain(dve.tensor_tensor(cat_rest[:, 1, :, :], cat_rest[:, 0, :, :], cat_part[:, :, 1, :], ALU.subtract))
            dve.tensor_copy(cat_part[:, :, 2, :], cat_rest[:, 1, :, :]).then_inc(parts_ready, 1)
            dve.wait_ge(params_ready, 2)
            dve.wait_ge(cur_ready, 1)
            dve.wait_ge(biases_ready, 2)
            dve.wait_ge(rows_known, 3)

            with dve.If(dve.value_load(most[0:1, 0:1], min_val=0, max_val=T) > P):
                dve.wait_ge(second_flipped, 1)
                dve.tensor_copy(slot_idx[:, :, 1, 0:P],
                                ps_z1[0][1][:, 0:2 * P].rearrange("p (k b) -> p k b", k=2)).then_inc(second_taken, 1)
                dve.tensor_copy(slot_mask[:, 1, 0:P], ps_z1[0][1][:, 2 * P:3 * P]).then_inc(second_taken, 1)
                dve.wait_ge(second_taken, 2)
                vector_loop(dve, HALVES)
            with dve.Else():
                vector_loop(dve, 1)

            moments(dve, chain, 2, [pooled_t[:, 0, :], pooled_t[:, 1, :]])
            norm_inputs(dve, chain, 2, [pooled_t[:, 0, :], pooled_t[:, 1, :]])

            def leaky(out_, in_):
                return dve.scalar_tensor_tensor(out=out_, in0=in_, scalar=0.1, in1=in_, op0=ALU.mult, op1=ALU.max)

            ps_y1 = [ps_z1[m // 2][m % 2][:, :] for m in range(4)]
            moments(dve, chain, 4, ps_y1[0:2], mlp1_done, 0)
            gains(dve, chain, 4, 2, bn1, 0, mb1)
            moments(dve, chain, 6, ps_y1[2:4], mlp1_done, 2)
            dve.wait_ge(normed, 1)
            leaky(x1[:, 0, :], y1[:, 0, :]).then_inc(x1_ready, 1)
            gains(dve, chain, 6, 2, bn1, 2, mb1)
            for m in range(1, 4):
                dve.wait_ge(normed, m + 1)
                leaky(x1[:, m, :], y1[:, m, :]).then_inc(x1_ready, 1)
            moments(dve, chain, 8, [ps_z2[:, :]], mlp2_done, 0)
            gains(dve, chain, 8, 1, bn2, 0, mb2)
            moments(dve, chain, 9, [ps_hist[:, :]], mlp2_done, 1)
            dve.wait_ge(normed, 5)
            leaky(x2[:, 0, :], y2[:, 0, :]).then_inc(x2_ready, 1)
            gains(dve, chain, 9, 1, bn2, 1, mb2)
            dve.wait_ge(normed, 6)
            leaky(x2[:, 1, :], y2[:, 1, :]).then_inc(x2_ready, 1)
            dve.wait_ge(mlp3_done, 1)
            for c in range(C):
                cols = slice(c * NOUT, (c + 1) * NOUT)
                chain(dve.tensor_tensor(half_out[:, c, :], ps_out[0][:, cols], mb3[:, :], ALU.add), c < C - 1)
            dve.wait_ge(mlp3_done, 2)
            dve.tensor_tensor(result[:, :, :], half_out[:, :, :],
                              ps_out[1][:, 0:C * NOUT].rearrange("p (c n) -> p c n", c=C),
                              ALU.add).then_inc(result_ready, 1)


_INS = ["r_uid", "r_mid", "r_cat", "r_historical_mid", "r_historical_cat", "r_mask"] + ["L0_rec_" + n for n in (
    "user_table", "mat_table", "cat_table", "lau_w1", "lau_b1", "lau_w2", "lau_b2", "lau_w3", "lau_b3", "bn0_g",
    "bn0_b", "mlp_w1", "mlp_b1", "bn1_g", "bn1_b", "mlp_w2", "mlp_b2", "bn2_g", "bn2_b", "mlp_w3", "mlp_b3")]


def kernel(**inputs):
    import numpy as np
    import concourse.bacc as bacc
    from concourse.bass_utils import run_bass_kernel_spmd

    nc = bacc.Bacc("TRN2", target_bir_lowering=False, num_devices=1)
    arrays, args = {}, []
    for name in _INS:
        a = np.ascontiguousarray(inputs[name])
        arrays[f"in_{name}"] = a
        args.append(nc.dram_tensor(f"in_{name}", a.shape, mybir.dt.from_np(a.dtype), kind="ExternalInput").ap())
    out = nc.dram_tensor("out", (B, NOUT), F32, kind="ExternalOutput").ap()
    rec_kernel(nc, *args, out)
    r = run_bass_kernel_spmd(nc, [arrays], core_ids=[0])
    return r.results[0]["out"]
```
